# Optimizing a Trainium2 kernel written in Bass

```python
import numpy as np
import jax
import jax.numpy as jnp

def _softmax(x, axis=-1):
    return jax.nn.softmax(x, axis=axis)

def _gelu(x):
    return jax.nn.gelu(x, approximate=True)

def _silu(x):
    return jax.nn.silu(x)

def _sigmoid(x):
    return jax.nn.sigmoid(x)

def _layernorm(x, axis=-1, eps=1e-05):
    m = jnp.mean(x, axis=axis, keepdims=True)
    v = jnp.var(x, axis=axis, keepdims=True)
    return (x - m) / jnp.sqrt(v + eps)

def _scatter_add(tgt, idx, src, axis=0):
    return tgt.at[idx].add(src)

def _segment_sum(src, seg, n):
    return jax.ops.segment_sum(src, seg, n)
kernel_name = 'mk_conv_attn_hybrid_d2_conv_nchw512_r2_37b21f'

def setup_inputs(seed: int=0):
    np.random.seed(seed)
    _w = jnp.asarray

    def _rec_inputs():
        import jax
        import jax.numpy as jnp
        _gk = jax.random.key(seed)
        x = -0.000125 + 0.9999 * jax.random.normal(jax.random.fold_in(_gk, 1), (16, 256, 32, 32), jnp.float32)
        return x
    x = _rec_inputs()

    def _L0_conv_setup():
        import jax, jax.numpy as jnp
        import numpy as np

        def conv1x1(x, W, b):
            return jnp.einsum('bchw,oc->bohw', x, W) + b[None, :, None, None]
        key = jax.random.key(seed)
        ks = jax.random.split(key, 10)
        B, C, H, W = (16, 256, 32, 32)
        c = C // 8
        s_in = 1.0 / np.sqrt(C)
        s_c = 1.0 / np.sqrt(c)
        return {'x': jax.random.normal(ks[0], (B, C, H, W), dtype=jnp.float32), 'Wq': jax.random.normal(ks[1], (c, C), dtype=jnp.float32) * s_in, 'bq': jax.random.normal(ks[2], (c,), dtype=jnp.float32) * 0.01, 'Wk': jax.random.normal(ks[3], (c, C), dtype=jnp.float32) * s_in, 'bk': jax.random.normal(ks[4], (c,), dtype=jnp.float32) * 0.01, 'Wv': jax.random.normal(ks[5], (c, C), dtype=jnp.float32) * s_in, 'bv': jax.random.normal(ks[6], (c,), dtype=jnp.float32) * 0.01, 'Wo': jax.random.normal(ks[7], (C, c), dtype=jnp.float32) * s_c, 'bo': jax.random.normal(ks[8], (C,), dtype=jnp.float32) * 0.01, 'gamma': jax.random.uniform(ks[9], (1,), dtype=jnp.float32)}
    _L0_conv_all = _L0_conv_setup()
    _L0_conv_in = {k: v for k, v in _L0_conv_all.items() if k in ('Wq', 'bq', 'Wk', 'bk', 'Wv', 'bv', 'Wo', 'bo', 'gamma')}
    del _L0_conv_all

    def _L1_attn_setup():
        import jax, jax.numpy as jnp
        import numpy as np
        B, S, D = (2, 1024, 256)
        H = 8
        G = 4
        LAMBDA_INIT = 0.2
        EPS = 1e-05
        key = jax.random.key(seed)
        ks = jax.random.split(key, 16)
        n = jax.random.normal
        return {'x': n(ks[0], (B, S, D), jnp.float32), 'K1_w': n(ks[1], (D, D), jnp.float32) * 0.02, 'K1_b': n(ks[2], (D,), jnp.float32) * 0.02, 'Q1_w': n(ks[3], (D, D), jnp.float32) * 0.02, 'K2_w': n(ks[4], (D, D), jnp.float32) * 0.02, 'K2_b': n(ks[5], (D,), jnp.float32) * 0.02, 'Q2_w': n(ks[6], (D, D), jnp.float32) * 0.02, 'V_w': n(ks[7], (D, D), jnp.float32) * 0.02, 'lambda_q1': n(ks[8], (H, 1), jnp.float32), 'lambda_k1': n(ks[9], (H, 1), jnp.float32), 'lambda_q2': n(ks[10], (H, 1), jnp.float32), 'lambda_k2': n(ks[11], (H, 1), jnp.float32), 'gn_w': jnp.ones((D,), jnp.float32), 'gn_b': jnp.zeros((D,), jnp.float32), 'out_w': n(ks[12], (D, D), jnp.float32) * 0.02, 'out_b': n(ks[13], (D,), jnp.float32) * 0.02}
    _L1_attn_all = _L1_attn_setup()
    _L1_attn_in = {k: v for k, v in _L1_attn_all.items() if k in ('K1_w', 'K1_b', 'Q1_w', 'K2_w', 'K2_b', 'Q2_w', 'V_w', 'lambda_q1', 'lambda_k1', 'lambda_q2', 'lambda_k2', 'gn_w', 'gn_b', 'out_w', 'out_b')}
    del _L1_attn_all

    def _L1_ffn_setup():
        import jax, jax.numpy as jnp
        import numpy as np
        B, T, D = (4, 512, 256)
        E, TOP_K, H = (8, 2, 128)
        key = jax.random.key(seed)
        ks = jax.random.split(key, 8)
        s = 0.02
        return {'x': jax.random.normal(ks[0], (B, T, D), dtype=jnp.float32), 'router': jax.random.normal(ks[1], (D, E), dtype=jnp.float32) * s, 'shared_gate': jax.random.normal(ks[2], (D, H), dtype=jnp.float32) * s, 'shared_up': jax.random.normal(ks[3], (D, H), dtype=jnp.float32) * s, 'shared_down': jax.random.normal(ks[4], (H, D), dtype=jnp.float32) * s, 'W_gate': jax.random.normal(ks[5], (E, D, H), dtype=jnp.float32) * s, 'W_up': jax.random.normal(ks[6], (E, D, H), dtype=jnp.float32) * s, 'W_down': jax.random.normal(ks[7], (E, H, D), dtype=jnp.float32) * s}
    _L1_ffn_all = _L1_ffn_setup()
    _L1_ffn_in = {k: v for k, v in _L1_ffn_all.items() if k in ('router', 'shared_gate', 'shared_up', 'shared_down', 'W_gate', 'W_up', 'W_down')}
    del _L1_ffn_all
    return {'x': x, 'L0_conv_Wq': _L0_conv_in['Wq'], 'L0_conv_bq': _L0_conv_in['bq'], 'L0_conv_Wk': _L0_conv_in['Wk'], 'L0_conv_bk': _L0_conv_in['bk'], 'L0_conv_Wv': _L0_conv_in['Wv'], 'L0_conv_bv': _L0_conv_in['bv'], 'L0_conv_Wo': _L0_conv_in['Wo'], 'L0_conv_bo': _L0_conv_in['bo'], 'L0_conv_gamma': _L0_conv_in['gamma'], 'L1_attn_K1_w': _L1_attn_in['K1_w'], 'L1_attn_K1_b': _L1_attn_in['K1_b'], 'L1_attn_Q1_w': _L1_attn_in['Q1_w'], 'L1_attn_K2_w': _L1_attn_in['K2_w'], 'L1_attn_K2_b': _L1_attn_in['K2_b'], 'L1_attn_Q2_w': _L1_attn_in['Q2_w'], 'L1_attn_V_w': _L1_attn_in['V_w'], 'L1_attn_lambda_q1': _L1_attn_in['lambda_q1'], 'L1_attn_lambda_k1': _L1_attn_in['lambda_k1'], 'L1_attn_lambda_q2': _L1_attn_in['lambda_q2'], 'L1_attn_lambda_k2': _L1_attn_in['lambda_k2'], 'L1_attn_gn_w': _L1_attn_in['gn_w'], 'L1_attn_gn_b': _L1_attn_in['gn_b'], 'L1_attn_out_w': _L1_attn_in['out_w'], 'L1_attn_out_b': _L1_attn_in['out_b'], 'L1_ffn_router': _L1_ffn_in['router'], 'L1_ffn_shared_gate': _L1_ffn_in['shared_gate'], 'L1_ffn_shared_up': _L1_ffn_in['shared_up'], 'L1_ffn_shared_down': _L1_ffn_in['shared_down'], 'L1_ffn_W_gate': _L1_ffn_in['W_gate'], 'L1_ffn_W_up': _L1_ffn_in['W_up'], 'L1_ffn_W_down': _L1_ffn_in['W_down']}

def reference(x, L0_conv_Wq, L0_conv_bq, L0_conv_Wk, L0_conv_bk, L0_conv_Wv, L0_conv_bv, L0_conv_Wo, L0_conv_bo, L0_conv_gamma, L1_attn_K1_w, L1_attn_K1_b, L1_attn_Q1_w, L1_attn_K2_w, L1_attn_K2_b, L1_attn_Q2_w, L1_attn_V_w, L1_attn_lambda_q1, L1_attn_lambda_k1, L1_attn_lambda_q2, L1_attn_lambda_k2, L1_attn_gn_w, L1_attn_gn_b, L1_attn_out_w, L1_attn_out_b, L1_ffn_router, L1_ffn_shared_gate, L1_ffn_shared_up, L1_ffn_shared_down, L1_ffn_W_gate, L1_ffn_W_up, L1_ffn_W_down):
    import jax
    import jax.numpy as jnp

    def _L0_conv_ref(x, Wq, bq, Wk, bk, Wv, bv, Wo, bo, gamma):
        import jax, jax.numpy as jnp
        import numpy as np

        def conv1x1(x, W, b):
            return jnp.einsum('bchw,oc->bohw', x, W) + b[None, :, None, None]
        B, C, H, W = x.shape
        c = Wq.shape[0]
        N = H * W
        queries = conv1x1(x, Wq, bq).reshape(B, c, N)
        keys = conv1x1(x, Wk, bk).reshape(B, N, c)
        attn = jax.nn.softmax(jnp.einsum('bcn,bnd->bcd', queries, keys), axis=-1)
        values = conv1x1(x, Wv, bv).reshape(B, c, N)
        out = jnp.einsum('bcd,bdn->bcn', attn, values).reshape(B, c, H, W)
        out = conv1x1(out, Wo, bo)
        return out * gamma + x

    def _L1_attn_ref(x, K1_w, K1_b, Q1_w, K2_w, K2_b, Q2_w, V_w, lambda_q1, lambda_k1, lambda_q2, lambda_k2, gn_w, gn_b, out_w, out_b):
        import jax, jax.numpy as jnp
        import numpy as np
        B, S, D = (2, 1024, 256)
        H = 8
        G = 4
        LAMBDA_INIT = 0.2
        EPS = 1e-05
        b, s, d = x.shape
        hd = d // H

        def heads(t):
            return t.reshape(b, s, H, hd).transpose(0, 2, 1, 3)
        q1 = heads(x @ Q1_w.T)
        k1 = heads(x @ K1_w.T + K1_b)
        q2 = heads(x @ Q2_w.T)
        k2 = heads(x @ K2_w.T + K2_b)
        v = heads(x @ V_w.T)
        scale = hd ** 0.5
        a1 = jax.nn.softmax(jnp.einsum('bhqd,bhkd->bhqk', q1, k1) / scale, axis=-1)
        a2 = jax.nn.softmax(jnp.einsum('bhqd,bhkd->bhqk', q2, k2) / scale, axis=-1)
        lam = jnp.exp(lambda_q1 * lambda_k1) - jnp.exp(lambda_q2 * lambda_k2) + LAMBDA_INIT
        attn = a1 - lam.reshape(1, H, 1, 1) * a2
        o = jnp.einsum('bhqk,bhkd->bhqd', attn, v)
        o = o.transpose(0, 2, 1, 3).reshape(b, s, d)
        xc = o.transpose(0, 2, 1).reshape(b, G, d // G, s)
        mu = xc.mean(axis=(2, 3), keepdims=True)
        var = xc.var(axis=(2, 3), keepdims=True)
        xn = ((xc - mu) * jax.lax.rsqrt(var + EPS)).reshape(b, d, s)
        xn = xn * gn_w[None, :, None] + gn_b[None, :, None]
        y = xn.transpose(0, 2, 1) @ out_w.T + out_b
        return y

    def _L1_ffn_ref(x, router, shared_gate, shared_up, shared_down, W_gate, W_up, W_down):
        import jax, jax.numpy as jnp
        import numpy as np
        B, T, D = (4, 512, 256)
        E, TOP_K, H = (8, 2, 128)
        b, t, d = x.shape
        n = b * t
        x_flat = x.reshape(n, d)
        shared_out = jax.nn.silu(x_flat @ shared_gate) * (x_flat @ shared_up) @ shared_down
        probs = jax.nn.softmax(x_flat @ router, axis=-1)
        topk_scores, topk_idx = jax.lax.top_k(probs, TOP_K)
        combine = jnp.zeros((n, E), dtype=x.dtype)
        combine = combine.at[jnp.arange(n)[:, None], topk_idx].set(topk_scores)
        gate = jax.nn.silu(jnp.einsum('nd,edh->enh', x_flat, W_gate))
        up = jnp.einsum('nd,edh->enh', x_flat, W_up)
        y = jnp.einsum('enh,ehd->end', gate * up, W_down)
        routed_out = jnp.einsum('ne,end->nd', combine, y)
        return (shared_out + routed_out).reshape(b, t, d)

    def _gn(v, G=32, eps=1e-05):
        B_, C_, H_, W_ = v.shape
        g = v.reshape(B_, G, C_ // G, H_, W_)
        m = jnp.mean(g, axis=(2, 3, 4), keepdims=True)
        s = jnp.var(g, axis=(2, 3, 4), keepdims=True)
        return ((g - m) / jnp.sqrt(s + eps)).reshape(v.shape)

    def _ln_c(v, eps=1e-06):
        m = jnp.mean(v, axis=1, keepdims=True)
        s = jnp.var(v, axis=1, keepdims=True)
        return (v - m) / jnp.sqrt(s + eps)

    def _ln_t(v, eps=1e-05):
        m = jnp.mean(v, axis=-1, keepdims=True)
        s = jnp.var(v, axis=-1, keepdims=True)
        return (v - m) / jnp.sqrt(s + eps)

    def _to_tokens(v):
        B_, C_, H_, W_ = v.shape
        return v.reshape(B_, C_, H_ * W_).transpose(0, 2, 1)

    def _from_tokens(t, like):
        B_, C_, H_, W_ = like.shape
        return t.transpose(0, 2, 1).reshape(B_, C_, H_, W_)
    x = _L0_conv_ref(x, L0_conv_Wq, L0_conv_bq, L0_conv_Wk, L0_conv_bk, L0_conv_Wv, L0_conv_bv, L0_conv_Wo, L0_conv_bo, L0_conv_gamma)
    t = _to_tokens(x)
    t = t + _L1_attn_ref(_ln_t(t), L1_attn_K1_w, L1_attn_K1_b, L1_attn_Q1_w, L1_attn_K2_w, L1_attn_K2_b, L1_attn_Q2_w, L1_attn_V_w, L1_attn_lambda_q1, L1_attn_lambda_k1, L1_attn_lambda_q2, L1_attn_lambda_k2, L1_attn_gn_w, L1_attn_gn_b, L1_attn_out_w, L1_attn_out_b)
    t = t + _L1_ffn_ref(_ln_t(t), L1_ffn_router, L1_ffn_shared_gate, L1_ffn_shared_up, L1_ffn_shared_down, L1_ffn_W_gate, L1_ffn_W_up, L1_ffn_W_down)
    x = _from_tokens(t, x)
    return x

_drawn_inputs = setup_inputs


def setup_inputs(seed=0):
    import zlib

    import numpy as np

    out = dict(_drawn_inputs(seed))
    spreads = {'L1_attn_gn_w': (1.0, 0.2), 'L1_attn_gn_b': (0.0, 0.318)}
    factors = {'L0_conv_bq': 2.896,
     'L0_conv_bk': 8.0,
     'L1_attn_K1_b': 8.0,
     'L1_attn_K2_b': 8.0,
     'L1_attn_out_b': 3.146,
     'L1_ffn_router': 8.0,
     'L1_ffn_shared_gate': 5.525,
     'L1_ffn_shared_up': 5.416,
     'L1_ffn_shared_down': 5.456,
     'L1_ffn_W_gate': 8.0,
     'L1_ffn_W_up': 8.0,
     'L1_ffn_W_down': 8.0}
    for name, (base, spread) in spreads.items():
        noise = np.random.default_rng([zlib.crc32(name.encode()), seed]).standard_normal(out[name].shape)
        drawn = base * np.exp(spread * noise) if base else spread * noise
        out[name] = jnp.asarray(drawn.astype(out[name].dtype))
    for name, factor in factors.items():
        out[name] = (out[name] * factor).astype(out[name].dtype)
    return out
```

```python
from contextlib import ExitStack

import numpy as np

import concourse.bass as bass
from concourse import mybir

F32 = mybir.dt.float32
F32R = mybir.dt.float32r
ACT = mybir.ActivationFunctionType
ALU = mybir.AluOpType
AX = mybir.AxisListType

P = 128
B, C, N = 16, 256, 1024
CT = C // P
NT = N // P
HALF = 512
NH = N // HALF
CR = 32
NJ = N // CR // 4
HEADS, HD = 8, 32
UNITS = 2 * HEADS
SCALE = float(HD) ** -0.5
E, HID = 8, 128
NE = E + 1
CQ = 256
AUX = 96
KS = AUX + 2
NST, NP = 3, 3
LN_EPS = 1e-5

W_QK = 0
W_V = W_QK + 4 * CT * C
W_O = W_V + CT * C
W_GU = W_O + CT * C
W_R = W_GU + NE * 2 * CT * HID
W_SEL = W_R + CT * E
W_SPLIT = W_SEL + E * P
F_QKV = 0
F_DOWN = F_QKV + CT * 3 * CR
F_WO = F_DOWN + NE * C
F_ID = F_WO + C
F_BLK = F_ID + P
F_IDX = F_BLK + P
F_VEC = F_IDX + NT * E
(V_BK, V_BV, V_BO, V_GAM, V_K1B, V_K2B, V_GNW, V_GNB, V_OUTB, V_LAM, V_BQ) = (
    0, 1, 2, 4, 5, 7, 9, 11, 13, 15, 47)
F_ALL = F_VEC + V_BQ + CR

FRONT = (2, 1, 2, 1, 2, 0, 0, 0)
T_AT = 6
PROJ_STEP = UNITS // 2 - 2


def ring_order():
    order = [("proj", t) for t in range(4)]
    order += [("score", 0, q) for q in range(NT)] + [("turn", 0)]
    for u in range(UNITS):
        if u == PROJ_STEP:
            order += [("proj", 4 + t) for t in range(4)]
        q = 0
        for kt in range(NT):
            if u + 1 < UNITS:
                order += [("score", u + 1, q + i) for i in range(FRONT[kt])]
                q += FRONT[kt]
                if kt == T_AT:
                    order.append(("turn", u + 1))
    return order


RING = ring_order()
RING_AT = {item: n for n, item in enumerate(RING)}
SLOT_USES = [len(range(s, UNITS, NST)) for s in range(NST)]
STACK_DMAS, AUX_DMAS = 5, 2
DVE_STEPS = 125


def build(nc, x, w_split, w_full, out):
    ctx = ExitStack()
    with ctx:
        def sb(name, shape, dt=F32):
            return ctx.enter_context(nc.sbuf_tensor(name, shape, dt))

        def sem(name):
            return ctx.enter_context(nc.semaphore(name))

        wh = sb("w_hi", [P, W_SPLIT], F32R)
        wl = sb("w_lo", [P, W_SEL], F32R)
        wf = sb("w_full", [P, F_ALL])
        ones = sb("ones", [P, CR])
        gbo = sb("gamma_bo", [P, CT])
        nlam = sb("minus_lambda", [P, HEADS])
        xin = sb("x_tile", [P, CT, N])
        res = sb("residual", [P, CT, N])
        xh = sb("act_hi", [P, CT, N], F32R)
        xl = sb("act_lo", [P, CT, N], F32R)
        stage = sb("stage", [P, 2, 4, N])
        stack = sb("stack", [P, NST, 2, N], F32R)
        probs = sb("probs", [P, NP, N])
        vt = sb("v_tokens", [P, NT, C])
        ocm = sb("o_channels", [P, CT, N])
        oh = sb("o_head", [P, 2, CQ])
        rec = sb("recip_sum", [P, CQ])
        ot = sb("o_second", [P, CQ])
        comb_t = sb("combine_rows", [P, N], F32R)
        nm = sb("minus_max", [P, 2, NT])
        mrow = sb("max_rows", [NT, 2, 2, P], F32R)
        small = sb("small", [P, 160])
        route = sb("route", [P, 6, NT * E])

        flat = stage[:, :, :, :].rearrange("p a t n -> p (a t n)")
        xt = flat[:, 0:NT * C].rearrange("p (t c) -> p t c", t=NT)
        qt_sb = flat[:, 2048:2048 + NJ * CR].rearrange("p (j c) -> p j c", j=NJ)
        k4_sb = flat[:, 2304:2304 + NJ * CR].rearrange("p (j c) -> p j c", j=NJ)
        a2_sb = flat[0:CR, 2560:2560 + C]
        at_sb = flat[0:CR, 2816:2816 + 5 * CR].rearrange("p (a c) -> p a c", a=5)
        v_sb = flat[0:CR, 3072:3072 + N]
        on_sb = flat[:, 0:CT * N].rearrange("p (t n) -> p t n", t=CT)
        th = flat[:, 0:2 * HALF].rearrange("p (s n) -> p s n", s=2)
        hid = flat[:, 1024:1024 + 2 * HALF].rearrange("p (s n) -> p s n", s=2)
        gu = flat[:, 2048:2048 + HALF]
        guu = flat[:, 2560:2560 + HALF]

        ps = ctx.enter_context(nc.psum_tensor("psum", [P, 8, HALF], F32))

        def wide(slot):
            return ps[:, 2 * slot:2 * slot + 2, :]

        def ident():
            return wf[:, F_ID:F_ID + P]

        def vec(c, n=1, rows=P):
            return wf[0:rows, F_VEC + c:F_VEC + c + n]

        raw_in, full_in, setup = sem("raw_weights_in"), sem("full_weights_in"), sem("setup_done")
        setup_step = sem("setup_step")
        sel_in, filled = sem("selectors_in"), sem("constants_filled")
        x_in, x_used, y_out = sem("x_in"), sem("x_used"), sem("y_out")
        step = sem("dve_step")
        c_full, c_ready, c_max, c_exp = sem("conv_filled"), sem("conv_ready"), sem("conv_max"), sem("conv_exp")
        t_full, t_var, t_sd, t_rs = sem("tokens_filled"), sem("ln_var"), sem("ln_sd"), sem("ln_rstd")
        n_act, n_dve = sem("ln_normed_act"), sem("ln_normed_dve")
        back_full, back_hi, back_lo = sem("back_filled"), sem("back_hi"), sem("back_lo")
        v_full, v_ready = sem("v_filled"), sem("v_ready")
        ring_full, ring_free = sem("ring_filled"), sem("ring_free")
        proj_hi = sem("proj_hi")
        stack_in = [sem(f"stack_in{s}") for s in range(NST)]
        aux_in = [sem(f"aux_in{s}") for s in range(NST)]
        st_full, p_ready, pv_done = sem("st_filled"), sem("probs_ready"), sem("pv_done")
        o_free, oh_ready = sem("o_free"), sem("o_head_ready")
        o_in = [sem(f"o_in{s}") for s in range(2)]
        g_stat, g_full, g_var, g_sd = sem("gn_stat"), sem("gn_filled"), sem("gn_var"), sem("gn_sd")
        on_ready, on_hi, on_lo = sem("on_ready"), sem("on_hi"), sem("on_lo")
        y1_full, y1_ready = sem("y1_filled"), sem("y1_ready")
        r_full, r_z, r_exp, r_comb = sem("router_filled"), sem("router_z"), sem("router_exp"), sem("combine_ready")
        cb_full, cb_hi, cb_lo = sem("combine_filled"), sem("combine_hi"), sem("combine_lo")
        f_full, f_th, f_hid, f_down, f_out = (
            sem("ffn_filled"), sem("ffn_tanh"), sem("ffn_hidden"), sem("ffn_down"), sem("ffn_out"))

        block = ctx.enter_context(nc.Block())

        @block.sync
        def _(sp):
            sp.dma_start(wf[:, :], w_full).then_inc(full_in, 16)
            sp.dma_start(flat[:, 0:W_SEL], w_split[:, 0:W_SEL]).then_inc(raw_in, 16)
            sp.dma_start(res[:, 0, :], w_split[:, W_SEL:W_SPLIT]).then_inc(sel_in, 16)
            sp.dma_start(xin[:, :, :], x[0].rearrange("(t p) n -> p t n", p=P)).then_inc(x_in, 16)

            def batch(b, more):
                def load_stack(u):
                    if u % 8 == 0:
                        sp.wait_ge(ring_free, b * len(RING) + RING_AT["proj", 4 * (u // 8) + 3] + 1)
                    elif u >= NST:
                        sp.wait_ge(pv_done, b * UNITS * NT + (u - NST + 1) * NT)
                    s, rows, m = u % NST, slice(HD * (u // 2 % 4), HD * (u // 2 % 4) + HD), u % 2
                    st = stack[:, s, :, :].bitcast(F32)
                    parts = ((st[0:HD, :, :], stage[rows, 0, 2 * m:2 * m + 2, :]),
                             (st[HD:2 * HD, 0, :], stage[rows, 1, 2 * m, :]),
                             (st[HD:2 * HD, 1, :], stage[rows, 0, 2 * m + 1, :]),
                             (st[2 * HD:3 * HD, 0, :], stage[rows, 0, 2 * m, :]),
                             (st[2 * HD:3 * HD, 1, :], stage[rows, 1, 2 * m + 1, :]))
                    for dst, src in parts:
                        sp.dma_start(dst, src).then_inc(stack_in[s], 16)

                def load_aux(u):
                    sp.wait_ge(ring_free, b * len(RING) + RING_AT["turn", u] + 1)
                    for part in range(2):
                        sp.dma_start(stack[AUX + part:AUX + part + 1, u % NST, 0, :].bitcast(F32)
                                     .rearrange("p (t n) -> p t n", t=NT),
                                     mrow[:, u % 2, part, :].bitcast(F32)).then_inc(aux_in[u % NST], 16)

                def save_head(h):
                    sp.wait_ge(oh_ready, b * HEADS + h + 1)
                    for c in range(4):
                        sp.dma_start(ocm[HD * (h % 4):HD * (h % 4) + HD, h // 4, c * CQ:(c + 1) * CQ],
                                     oh[HD * c:HD * c + HD, h % 2, :]).then_inc(o_in[h % 2], 16)

                if more:
                    sp.wait_ge(x_used, b * 4 + 4)
                    sp.dma_start(xin[:, :, :], x[b + 1].rearrange("(t p) n -> p t n", p=P)).then_inc(x_in, 16)
                load_stack(0)
                load_stack(1)
                load_aux(0)
                load_stack(2)
                for u in range(UNITS):
                    if u + 1 < UNITS:
                        load_aux(u + 1)
                    if u % 2 == 0 and u:
                        save_head(u // 2 - 1)
                    if u + NST < UNITS:
                        load_stack(u + NST)
                save_head(HEADS - 1)
                for half in range(NH):
                    sp.wait_ge(f_out, b * NH * CT + NH * CT + CT * (half + 1))
                    cols = slice(half * HALF, (half + 1) * HALF)
                    sp.dma_start(out[b].rearrange("(t p) n -> p t n", p=P)[:, :, cols],
                                 res[:, :, cols]).then_inc(y_out, 16)

            with sp.Fori(0, B - 1) as b:
                batch(b, True)
            batch(B - 1, False)
            sp.wait_ge(y_out, (B + 1) * NH * 16)

        @block.gpsimd
        def _(pool):
            nc.gpsimd.memset(ones[:, :], 1.0).then_inc(filled, 1)
            pool.wait_ge(filled, 1)
            nc.gpsimd.memset(stack[AUX:P, :, 1, :].bitcast(F32), 1.0).then_inc(filled, 1)
            pool.wait_ge(filled, 2)
            nc.gpsimd.memset(comb_t[:, :].bitcast(F32), 0.0).then_inc(filled, 1)

        @block.scalar
        def _(act):
            act.wait_ge(raw_in, 16)
            nc.scalar.activation(wh[:, 0:W_SEL], flat[:, 0:W_SEL], ACT.Copy).then_inc(setup, 1)
            act.wait_ge(sel_in, 16)
            nc.scalar.activation(wh[:, W_SEL:W_SPLIT], res[:, 0, :], ACT.Copy).then_inc(setup, 1)
            act.wait_ge(full_in, 16)
            act.wait_ge(setup_step, 2)
            nc.scalar.activation(small[:, 16:32], small[:, 0:16], ACT.Exp).then_inc(setup_step, 1)
            with act.Fori(0, B) as b:
                act.wait_ge(c_max, b + 1)
                nc.scalar.activation(at_sb[:, 0, :], ps[0:CR, 4, 0:CR], ACT.Exp, bias=small[0:CR, 32:33],
                                     accum_out=small[0:CR, 33:34]).then_inc(c_exp, 1)

                def layer_norm(i):
                    act.wait_ge(t_var, b * 2 + i + 1)
                    nc.scalar.activation(small[:, 64:72], small[:, 56:64], ACT.Sqrt).then_inc(t_sd, 1)
                    act.wait_ge(t_rs, b * 2 + i + 1)
                    for k in range(2):
                        for tt in (2 * k, 2 * k + 1):
                            last = nc.scalar.activation(
                                xt[:, tt, :], ps[:, 4 + k, (tt % 2) * C:(tt % 2 + 1) * C], ACT.Identity,
                                bias=small[:, 80 + tt:81 + tt], scale=small[:, 72 + tt:73 + tt])
                        last.then_inc(n_act, 1)
                    for k in range(4):
                        act.wait_ge(back_full, b * 8 + 4 * i + k + 1)
                        cols = slice((k % 2) * HALF, (k % 2 + 1) * HALF)
                        nc.scalar.activation(xh[:, k // 2, cols], ps[:, k, :], ACT.Copy).then_inc(back_hi, 1)

                layer_norm(0)
                for k in range(4):
                    act.wait_ge(v_full, b * 4 + k + 1)
                    nc.scalar.activation(vt[:, 2 * k:2 * k + 2, :],
                                         ps[:, 4 + k, :].rearrange("p (t c) -> p t c", t=2),
                                         ACT.Copy).then_inc(v_ready, 1)

                def project(g):
                    for t in range(4):
                        n = RING_AT["proj", 4 * g + t]
                        act.wait_ge(ring_full, b * len(RING) + n + 1)
                        if g and t == 0:
                            for s in range(NST):
                                done = len(range(s, 8, NST))
                                act.wait_ge(stack_in[s], (b * SLOT_USES[s] + done) * STACK_DMAS * 16)
                        dst = stage[:, 0, t, :].bitcast(F32R)
                        src = wide(n % 2).rearrange("p h n -> p (h n)")
                        if t % 2 == 0:
                            ins = nc.scalar.activation(dst, src, ACT.Copy, scale=SCALE)
                        else:
                            ins = nc.scalar.activation(dst, src, ACT.Identity,
                                                       bias=vec((V_K1B, V_K2B)[t // 2] + g))
                        ins.then_inc(proj_hi, 1)

                project(0)
                for u in range(UNITS):
                    if u == PROJ_STEP:
                        project(1)
                    for kt in range(NT):
                        k = u * NT + kt
                        if k >= NP:
                            act.wait_ge(pv_done, b * UNITS * NT + k - NP + 1)
                        for half in range(2):
                            act.wait_ge(st_full, b * 2 * UNITS * NT + 2 * k + half + 1)
                            nc.scalar.activation(probs[:, k % NP, half * HALF:(half + 1) * HALF],
                                                 ps[:, 4 + half, :], ACT.Exp).then_inc(p_ready, 1)
                act.wait_ge(g_var, b + 1)
                nc.scalar.activation(small[:, 104:106], small[:, 102:104], ACT.Sqrt).then_inc(g_sd, 1)
                for t in range(CT):
                    act.wait_ge(on_ready, b * CT + t + 1)
                    nc.scalar.activation(xh[:, t, :], on_sb[:, t, :], ACT.Copy).then_inc(on_hi, 1)
                layer_norm(1)
                act.wait_ge(r_z, b + 1)
                nc.scalar.activation(route[:, 1, :], route[:, 0, :], ACT.Exp).then_inc(r_exp, 1)
                for i in range(NH * NE):
                    if i == 1:
                        act.wait_ge(cb_full, b + 1)
                        nc.scalar.activation(comb_t[0:E, :], ps[0:E, 6:8, :].rearrange("p h n -> p (h n)"),
                                             ACT.Copy).then_inc(cb_hi, 1)
                    act.wait_ge(f_full, b * NH * NE + i + 1)
                    if i >= 2:
                        act.wait_ge(f_hid, b * NH * NE + i - 1)
                    nc.scalar.activation(th[:, i % 2, :], ps[:, 2 + 3 * (i % 2), :], ACT.Tanh,
                                         scale=0.5).then_inc(f_th, 1)

        @block.vector
        def _(dve):
            v = nc.vector
            dve.wait_ge(full_in, 16)
            lam = wf[:, F_VEC + V_LAM:F_VEC + V_LAM + 32].rearrange("p (m a h) -> p m a h", m=2, a=2)
            for m in range(2):
                v.tensor_tensor(small[:, 8 * m:8 * m + 8], lam[:, m, 0, :], lam[:, m, 1, :],
                                ALU.mult).then_inc(setup_step, 1)
            v.tensor_scalar(gbo[:, :], vec(V_BO, 2), vec(V_GAM), None, ALU.mult).then_inc(setup, 1)
            dve.wait_ge(setup_step, 3)
            v.tensor_tensor(small[:, 40:48], small[:, 24:32], small[:, 16:24], ALU.subtract).then_inc(setup_step, 1)
            dve.wait_ge(setup_step, 4)
            v.tensor_scalar(nlam[:, :], small[:, 40:48], -0.2, None, ALU.add).then_inc(setup, 1)
            dve.wait_ge(setup, 4)
            v.tensor_tensor(wl[:, :], flat[:, 0:W_SEL], wh[:, 0:W_SEL], ALU.subtract).then_inc(setup, 1)
            dve.wait_ge(setup, 5)
            v.memset(small[:, 0:1], 0.0).then_inc(f_out, NH * CT)
            v.memset(small[:, 1:2], 0.0).then_inc(y_out, NH * 16)

            with dve.Fori(0, B) as b:
                taken = [0]

                def link(ins):
                    taken[0] += 1
                    ins.then_inc(step, 1)
                    dve.wait_ge(step, b * DVE_STEPS + taken[0])

                dve.wait_ge(c_full, b * 7 + 1)
                v.tensor_tensor(qt_sb, ps[:, 0, 0:NJ * CR].rearrange("p (j c) -> p j c", j=NJ),
                                vec(V_BQ, CR).unsqueeze(1).broadcast_to([P, NJ, CR]), ALU.add)
                v.tensor_scalar(k4_sb, ps[:, 1, 0:NJ * CR].rearrange("p (j c) -> p j c", j=NJ),
                                vec(V_BK), None, ALU.add)
                v.tensor_scalar(v_sb, ps[0:CR, 2:4, :].rearrange("p h n -> p (h n)"),
                                vec(V_BV, rows=CR), None, ALU.add).then_inc(c_ready, 1)
                dve.wait_ge(c_full, b * 7 + 2)
                v.tensor_reduce(small[0:CR, 32:33], ps[0:CR, 4, 0:CR], AX.X, ALU.max, negate=True).then_inc(c_max, 1)
                dve.wait_ge(c_exp, b + 1)
                link(v.reciprocal(small[0:CR, 34:35], small[0:CR, 33:34]))
                v.tensor_scalar(at_sb[:, 1:5, :], at_sb[:, 0:1, :].broadcast_to([CR, 4, CR]), small[0:CR, 34:35],
                                None, ALU.mult).then_inc(c_ready, 1)
                dve.wait_ge(c_full, b * 7 + 3)
                v.tensor_scalar(a2_sb, ps[0:CR, 5, 0:C], vec(V_GAM, rows=CR), None, ALU.mult).then_inc(c_ready, 1)
                dve.wait_ge(y_out, b * NH * 16 + NH * 16)
                for k in range(4):
                    t, cols = k // 2, slice((k % 2) * HALF, (k % 2 + 1) * HALF)
                    dve.wait_ge(c_full, b * 7 + 4 + k)
                    v.scalar_tensor_tensor(res[:, t, cols], ps[:, k, :], gbo[:, t:t + 1], xin[:, t, cols],
                                           ALU.add, ALU.add).then_inc(x_used, 1)

                def layer_norm(i):
                    for k in range(4):
                        dve.wait_ge(t_full, b * 8 + 4 * i + k + 1)
                        for tt in (2 * k, 2 * k + 1):
                            v.bn_stats(small[:, 112 + 6 * (tt % 8):118 + 6 * (tt % 8)],
                                       ps[:, 4 + k, (tt % 2) * C:(tt % 2 + 1) * C]).then_inc(step, 1)
                            taken[0] += 1
                    dve.wait_ge(step, b * DVE_STEPS + taken[0])
                    even, odd = small[:, 113:160:6], small[:, 116:160:6]
                    link(v.tensor_tensor(small[:, 40:48], even, odd, ALU.add))
                    v.tensor_tensor(small[:, 48:56], small[:, 114:160:6], small[:, 117:160:6],
                                    ALU.add).then_inc(step, 1)
                    taken[0] += 1
                    link(v.tensor_tensor(small[:, 88:96], even, odd, ALU.subtract))
                    link(v.scalar_tensor_tensor(small[:, 88:96], small[:, 88:96], 0.25, small[:, 88:96],
                                                ALU.mult, ALU.mult))
                    link(v.tensor_scalar(small[:, 48:56], small[:, 48:56], 1.0 / C, LN_EPS, ALU.mult, ALU.add))
                    v.tensor_tensor(small[:, 56:64], small[:, 48:56], small[:, 88:96], ALU.add).then_inc(t_var, 1)
                    dve.wait_ge(t_sd, b * 2 + i + 1)
                    link(v.reciprocal(small[:, 72:80], small[:, 64:72]))
                    v.scalar_tensor_tensor(small[:, 80:88], small[:, 40:48], -0.5, small[:, 72:80],
                                           ALU.mult, ALU.mult).then_inc(t_rs, 1)
                    dve.wait_ge(t_rs, b * 2 + i + 1)
                    for k in range(2, 4):
                        for tt in (2 * k, 2 * k + 1):
                            last = v.tensor_scalar(xt[:, tt, :], ps[:, 4 + k, (tt % 2) * C:(tt % 2 + 1) * C],
                                                   small[:, 72 + tt:73 + tt], small[:, 80 + tt:81 + tt],
                                                   ALU.mult, ALU.add)
                        last.then_inc(n_dve, 1)
                    for k in range(4):
                        cols = slice((k % 2) * HALF, (k % 2 + 1) * HALF)
                        dve.wait_ge(back_hi, b * 8 + 4 * i + k + 1)
                        v.tensor_tensor(xl[:, k // 2, cols], ps[:, k, :], xh[:, k // 2, cols],
                                        ALU.subtract).then_inc(back_lo, 1)

                layer_norm(0)

                def ring_step(item):
                    n = RING_AT[item]
                    dve.wait_ge(ring_full, b * len(RING) + n + 1)
                    flat_in = wide(n % 2).rearrange("p h n -> p (h n)")
                    if item[0] == "proj":
                        t = item[1] % 4
                        dve.wait_ge(proj_hi, b * 8 + item[1] + 1)
                        dst, hi = stage[:, 1, t, :].bitcast(F32R), stage[:, 0, t, :]
                        bias = vec((V_K1B, V_K2B)[t // 2] + item[1] // 4)
                        v.scalar_tensor_tensor(dst, flat_in, SCALE if t % 2 == 0 else bias, hi,
                                               ALU.mult if t % 2 == 0 else ALU.add,
                                               ALU.subtract).then_inc(ring_free, 1)
                    elif item[0] == "score":
                        _, u, q = item
                        v.tensor_reduce(nm[:, u % 2, q:q + 1], flat_in, AX.X, ALU.max,
                                        negate=True).then_inc(ring_free, 1)
                    else:
                        u = item[1]
                        if u >= 2:
                            s = (u - 2) % NST
                            dve.wait_ge(aux_in[s], (b * SLOT_USES[s] + (u - 2) // NST + 1) * AUX_DMAS * 16)
                        rows = ps[0:NT, 2 * (n % 2), 0:P]
                        link(v.tensor_copy(mrow[:, u % 2, 0, :], rows))
                        v.tensor_tensor(mrow[:, u % 2, 1, :], rows, mrow[:, u % 2, 0, :],
                                        ALU.subtract).then_inc(ring_free, 1)

                def head_out(u):
                    h = u // 2
                    dve.wait_ge(pv_done, b * UNITS * NT + (u + 1) * NT)
                    bank = 6 + u % 2
                    if u:
                        dve.wait_ge(o_free, b * UNITS + u)
                    link(v.reciprocal(rec[:, :], ps[:, bank, CQ:2 * CQ]))
                    if u % 2 == 0:
                        if h >= 2:
                            dve.wait_ge(o_in[h % 2], (b * (HEADS // 2) + h // 2) * 4 * 16)
                        v.tensor_tensor(oh[:, h % 2, :], ps[:, bank, 0:CQ], rec[:, :], ALU.mult).then_inc(o_free, 1)
                    else:
                        v.scalar_tensor_tensor(ot[:, :], ps[:, bank, 0:CQ], nlam[:, h:h + 1], rec[:, :],
                                               ALU.mult, ALU.mult).then_inc(o_free, 1)
                        dve.wait_ge(o_free, b * UNITS + u + 1)
                        v.tensor_tensor(oh[:, h % 2, :], oh[:, h % 2, :], ot[:, :], ALU.add).then_inc(oh_ready, 1)

                for item in RING[:RING_AT["turn", 0] + 1]:
                    ring_step(item)
                for u in range(UNITS):
                    if u == PROJ_STEP:
                        for t in range(4):
                            ring_step(("proj", 4 + t))
                    if u + 1 < UNITS:
                        for q in range(3):
                            ring_step(("score", u + 1, q))
                    if u:
                        head_out(u - 1)
                    if u + 1 < UNITS:
                        for q in range(3, NT):
                            ring_step(("score", u + 1, q))
                        ring_step(("turn", u + 1))
                head_out(UNITS - 1)

                for s in range(2):
                    dve.wait_ge(o_in[s], (b + 1) * (HEADS // 2) * 4 * 16)
                for t in range(CT):
                    for half in range(NH):
                        v.bn_stats(small[:, 112 + 12 * t + 6 * half:118 + 12 * t + 6 * half],
                                   ocm[:, t, half * HALF:(half + 1) * HALF]).then_inc(step, 1)
                        taken[0] += 1
                dve.wait_ge(step, b * DVE_STEPS + taken[0])
                means = small[:, 113:136:3]
                g_mean, g_sq = small[:, 0:8], small[:, 8:16]
                v.tensor_copy(g_mean, means).then_inc(step, 1)
                taken[0] += 1
                link(v.tensor_tensor(small[:, 16:24], means, means, ALU.mult))
                link(v.scalar_tensor_tensor(g_sq, small[:, 114:136:3], 4.0 / N, small[:, 16:24],
                                            ALU.mult, ALU.add))
                v.tensor_reduce(small[:, 92:96], small[:, 0:16].rearrange("p (a n) -> p a n", n=4), AX.X,
                                ALU.add).then_inc(g_stat, 1)
                dve.wait_ge(g_full, b + 1)
                link(v.tensor_copy(small[:, 96:100], ps[:, 0, 0:4]))
                link(v.tensor_tensor(small[:, 100:102], small[:, 96:98], small[:, 96:98], ALU.mult))
                link(v.tensor_tensor(small[:, 100:102], small[:, 98:100], small[:, 100:102], ALU.subtract))
                v.tensor_scalar(small[:, 102:104], small[:, 100:102], LN_EPS, None, ALU.add).then_inc(g_var, 1)
                dve.wait_ge(g_sd, b + 1)
                link(v.reciprocal(small[:, 106:108], small[:, 104:106]))
                link(v.tensor_tensor(small[:, 106:108], small[:, 106:108], vec(V_GNW, 2), ALU.mult))
                link(v.tensor_tensor(small[:, 108:110], small[:, 96:98], small[:, 106:108], ALU.mult))
                link(v.tensor_tensor(small[:, 108:110], vec(V_GNB, 2), small[:, 108:110], ALU.subtract))
                for t in range(CT):
                    v.tensor_scalar(on_sb[:, t, :], ocm[:, t, :], small[:, 106 + t:107 + t],
                                    small[:, 108 + t:109 + t], ALU.mult, ALU.add).then_inc(on_ready, 1)
                for t in range(CT):
                    dve.wait_ge(on_hi, b * CT + t + 1)
                    v.tensor_tensor(xl[:, t, :], on_sb[:, t, :], xh[:, t, :], ALU.subtract).then_inc(on_lo, 1)
                for k in range(4):
                    t, cols = k // 2, slice((k % 2) * HALF, (k % 2 + 1) * HALF)
                    dve.wait_ge(y1_full, b * 4 + k + 1)
                    v.scalar_tensor_tensor(res[:, t, cols], ps[:, k, :], vec(V_OUTB + t), res[:, t, cols],
                                           ALU.add, ALU.add).then_inc(y1_ready, 1)
                layer_norm(1)

                def r3(i):
                    return route[:, i, :].rearrange("p (t e) -> p t e", t=NT)

                def wide8(col):
                    return small[:, col:col + NT].unsqueeze(2).broadcast_to([P, NT, E])

                dve.wait_ge(r_full, b + 1)
                lg = ps[:, 0, 0:NT * E].rearrange("p (t e) -> p t e", t=NT)
                link(v.tensor_reduce(small[:, 0:8], lg, AX.X, ALU.max, negate=True))
                v.tensor_tensor(r3(0), lg, wide8(0), ALU.add).then_inc(r_z, 1)
                dve.wait_ge(r_exp, b + 1)
                link(v.tensor_reduce(small[:, 0:8], r3(1), AX.X, ALU.add))
                link(v.reciprocal(small[:, 8:16], small[:, 0:8]))
                link(v.tensor_tensor(r3(0), r3(1), wide8(8), ALU.mult))
                idx = wf[:, F_IDX:F_IDX + NT * E].rearrange("p (t e) -> p t e", t=NT)
                source = 0
                for rank in range(2):
                    link(v.tensor_reduce(small[:, 0:8], r3(source), AX.X, ALU.max))
                    link(v.tensor_tensor(r3(1), r3(source), wide8(0), ALU.is_equal))
                    link(v.tensor_tensor(r3(1), r3(1), idx, ALU.mult))
                    link(v.tensor_reduce(small[:, 8:16], r3(1), AX.X, ALU.max))
                    link(v.tensor_tensor(r3(2 + rank), r3(1), wide8(8), ALU.is_equal))
                    if rank == 0:
                        link(v.scalar_tensor_tensor(r3(4), r3(2), -2.0, r3(0), ALU.mult, ALU.add))
                        source = 4
                link(v.tensor_tensor(r3(2), r3(2), r3(3), ALU.add))
                v.tensor_tensor(r3(5), r3(2), r3(0), ALU.mult).then_inc(r_comb, 1)

                for i in range(NH * NE):
                    half, e = divmod(i, NE)
                    if i == 1:
                        dve.wait_ge(cb_hi, b + 1)
                        v.tensor_tensor(comb_t[32:32 + E, :], ps[0:E, 6:8, :].rearrange("p h n -> p (h n)"),
                                        comb_t[0:E, :], ALU.subtract).then_inc(cb_lo, 1)
                    bank = 2 + 3 * (i % 2)
                    dve.wait_ge(f_th, b * NH * NE + i + 1)
                    if i:
                        dve.wait_ge(f_hid, b * NH * NE + i)
                    link(v.scalar_tensor_tensor(gu, th[:, i % 2, :], 1.0, ps[:, bank, :], ALU.add, ALU.mult))
                    if i >= 2:
                        dve.wait_ge(f_down, b * NH * NE + i - 1)
                    if e == 0:
                        v.scalar_tensor_tensor(hid[:, i % 2, :], gu, 0.5, ps[:, bank + 1, :],
                                               ALU.mult, ALU.mult).then_inc(f_hid, 1)
                    else:
                        link(v.tensor_tensor(guu, gu, ps[:, bank + 1, :], ALU.mult))
                        v.tensor_tensor(hid[:, i % 2, :], guu, ps[:, bank + 2, :], ALU.mult).then_inc(f_hid, 1)
                    if e == NE - 1:
                        dve.wait_ge(f_down, b * NH * NE + i + 1)
                        for t in range(CT):
                            cols = slice(half * HALF, (half + 1) * HALF)
                            v.tensor_tensor(res[:, t, cols], ps[:, t, :], res[:, t, cols],
                                            ALU.add).then_inc(f_out, 1)
                assert taken[0] == DVE_STEPS, taken[0]

        @block.tensor
        def _(pe):
            mm = nc.tensor.matmul

            def split_mm(dst, w, wn, act_cols, first=True, last=True):
                n, ins = 0, None
                for kt in range(CT):
                    for wt, xx in ((wh, xh), (wl, xh), (wh, xl)):
                        ins = mm(dst, wt[:, w + kt * wn[0]:w + kt * wn[0] + wn[1]], xx[:, kt, act_cols],
                                 start=(first and n == 0), stop=(last and n == 3 * CT - 1))
                        n += 1
                return ins

            pe.wait_ge(full_in, 16)
            pe.wait_ge(setup, 5)
            pe.wait_ge(filled, 3)
            with pe.Fori(0, B) as b:
                pe.wait_ge(x_in, b * 16 + 16)
                pe.wait_ge(f_out, b * NH * CT + NH * CT)
                xq = xin[:, :, :].rearrange("p t (c j q) -> p t j q c", c=CR, j=NJ)
                xk = xin[:, :, :].rearrange("p t (j q d) -> p t q j d", q=4, d=CR)
                wq = wf[:, F_QKV:F_QKV + CT * 3 * CR].rearrange("p (t w c) -> p t w c", t=CT, w=3)
                for j in range(NJ):
                    for kt in range(CT):
                        for q in range(4):
                            mm(ps[CR * q:CR * q + CR, 0, j * CR:(j + 1) * CR], xq[:, kt, j, q, :], wq[:, kt, 0, :],
                               start=(kt == 0), stop=(kt == CT - 1))
                for q in range(4):
                    for kt in range(CT):
                        mm(ps[CR * q:CR * q + CR, 1, 0:NJ * CR], wq[:, kt, 1, :], xk[:, kt, q, :, :],
                           start=(kt == 0), stop=(kt == CT - 1))
                for half in range(NH):
                    for kt in range(CT):
                        last = mm(ps[0:CR, 2 + half, :], wq[:, kt, 2, :],
                                  xin[:, kt, half * HALF:(half + 1) * HALF], start=(kt == 0), stop=(kt == CT - 1))
                last.then_inc(c_full, 1)
                pe.wait_ge(c_ready, b * 3 + 1)
                for j in range(NJ):
                    last = mm(ps[0:CR, 4, 0:CR], qt_sb[:, j, :], k4_sb[:, j, :], start=(j == 0), stop=(j == NJ - 1))
                last.then_inc(c_full, 1)
                pe.wait_ge(c_ready, b * 3 + 2)
                mm(ps[:, 5, 0:C], at_sb[:, 1:5, :].rearrange("p a c -> p (a c)"), wf[0:CR, F_WO:F_WO + C], start=True, stop=True).then_inc(c_full, 1)
                pe.wait_ge(c_ready, b * 3 + 3)
                for k in range(4):
                    mm(ps[:, k, :], a2_sb[:, (k // 2) * P:(k // 2 + 1) * P], v_sb[:, (k % 2) * HALF:(k % 2 + 1) * HALF],
                       start=True, stop=True).then_inc(c_full, 1)

                def layer_norm(i):
                    if i == 0:
                        pe.wait_ge(x_used, b * 4 + 4)
                    else:
                        pe.wait_ge(y1_ready, b * 4 + 4)
                    for tt in range(NT):
                        for ct in range(CT):
                            last = nc.tensor.transpose(ps[:, 4 + tt // 2, (tt % 2) * C + ct * P:(tt % 2) * C + ct * P + P],
                                                       res[:, ct, tt * P:(tt + 1) * P], ident())
                        if tt % 2:
                            last.then_inc(t_full, 1)
                    pe.wait_ge(n_act, b * 4 + 2 * i + 2)
                    pe.wait_ge(n_dve, b * 4 + 2 * i + 2)
                    for k in range(4):
                        for q in range(4):
                            tt = 4 * (k % 2) + q
                            last = nc.tensor.transpose(ps[:, k, q * P:(q + 1) * P],
                                                       xt[:, tt, (k // 2) * P:(k // 2 + 1) * P], ident())
                        last.then_inc(back_full, 1)
                    pe.wait_ge(back_lo, b * 8 + 4 * i + 4)

                layer_norm(0)
                for tt in range(NT):
                    n = 0
                    for kt in range(CT):
                        for xx, wt in ((xh, wh), (xh, wl), (xl, wh)):
                            last = mm(ps[:, 4 + tt // 2, (tt % 2) * C:(tt % 2 + 1) * C], xx[:, kt, tt * P:(tt + 1) * P],
                                      wt[:, W_V + kt * C:W_V + (kt + 1) * C], start=(n == 0), stop=(n == 5))
                            n += 1
                    if tt % 2:
                        last.then_inc(v_full, 1)

                def ring_step(item):
                    n = RING_AT[item]
                    if n >= 2:
                        pe.wait_ge(ring_free, b * len(RING) + n - 1)
                    slot = wide(n % 2)
                    if item[0] == "proj":
                        g, t = divmod(item[1], 4)
                        for half in range(NH):
                            last = split_mm(slot[:, half, :], W_QK + t * CT * C + g * P, (C, P),
                                            slice(half * HALF, (half + 1) * HALF))
                    elif item[0] == "score":
                        _, u, q = item
                        s = u % NST
                        if q == 0:
                            pe.wait_ge(stack_in[s], (b * SLOT_USES[s] + u // NST + 1) * STACK_DMAS * 16)
                        for half in range(NH):
                            last = mm(slot[:, half, :], stack[0:AUX, s, 0, q * P:(q + 1) * P],
                                      stack[0:AUX, s, 1, half * HALF:(half + 1) * HALF], start=True, stop=True)
                    else:
                        u = item[1]
                        pe.wait_ge(ring_free, b * len(RING) + RING_AT["score", u, NT - 1] + 1)
                        last = nc.tensor.transpose(slot[0:NT, 0, 0:P], nm[:, u % 2, :], ident())
                    last.then_inc(ring_full, 1)

                def weighted(u, kt):
                    h, k, bank = u // 2, u * NT + kt, 6 + u % 2
                    pe.wait_ge(p_ready, b * 2 * UNITS * NT + 2 * k + 2)
                    if kt == 0 and u >= 2:
                        pe.wait_ge(o_free, b * UNITS + u - 1)
                    for part in range(2):
                        for c in range(4):
                            lhs = vt[:, kt, HD * h:HD * h + HD] if part == 0 else ones[:, :]
                            last = mm(ps[HD * c:HD * c + HD, bank, part * CQ:(part + 1) * CQ], lhs,
                                      probs[:, k % NP, c * CQ:(c + 1) * CQ], start=(kt == 0 and part == 0),
                                      stop=(kt == NT - 1), skip_group_check=True)
                    last.then_inc(pv_done, 1)

                for item in RING[:RING_AT["turn", 0] + 1]:
                    ring_step(item)
                pe.wait_ge(v_ready, b * 4 + 4)
                for u in range(UNITS):
                    if u == PROJ_STEP:
                        for t in range(4):
                            ring_step(("proj", 4 + t))
                    s = u % NST
                    pe.wait_ge(aux_in[s], (b * SLOT_USES[s] + u // NST + 1) * AUX_DMAS * 16)
                    q = 0
                    for kt in range(NT):
                        k = u * NT + kt
                        for half in range(NH):
                            if k >= 1:
                                pe.wait_ge(p_ready, b * 2 * UNITS * NT + 2 * k + half - 1)
                            mm(ps[:, 4 + half, :], stack[0:KS, s, 1, kt * P:(kt + 1) * P],
                               stack[0:KS, s, 0, half * HALF:(half + 1) * HALF], start=True,
                               stop=True).then_inc(st_full, 1)
                        if u + 1 < UNITS:
                            for _ in range(FRONT[kt]):
                                ring_step(("score", u + 1, q))
                                q += 1
                        if k >= 1:
                            weighted(*divmod(k - 1, NT))
                        if u + 1 < UNITS and kt == T_AT:
                            ring_step(("turn", u + 1))
                weighted(UNITS - 1, NT - 1)

                pe.wait_ge(g_stat, b + 1)
                mm(ps[:, 0, 0:4], wf[:, F_BLK:F_BLK + P], small[:, 92:96], start=True, stop=True).then_inc(g_full, 1)
                pe.wait_ge(on_lo, b * CT + CT)
                for k in range(4):
                    split_mm(ps[:, k, :], W_O + (k // 2) * P, (C, P),
                             slice((k % 2) * HALF, (k % 2 + 1) * HALF)).then_inc(y1_full, 1)
                layer_norm(1)

                for tt in range(NT):
                    n = 0
                    for kt in range(CT):
                        for xx, wt in ((xh, wh), (xh, wl), (xl, wh)):
                            last = mm(ps[:, 0, tt * E:(tt + 1) * E], xx[:, kt, tt * P:(tt + 1) * P],
                                      wt[:, W_R + kt * E:W_R + (kt + 1) * E], start=(n == 0), stop=(n == 5))
                            n += 1
                last.then_inc(r_full, 1)

                def down(i):
                    half, e = divmod(i, NE)
                    pe.wait_ge(f_hid, b * NH * NE + i + 1)
                    if e == 0 and half:
                        pe.wait_ge(f_out, b * NH * CT + NH * CT + CT * half)
                    for t in range(CT):
                        last = mm(ps[:, t, :], wf[:, F_DOWN + e * C + t * P:F_DOWN + e * C + (t + 1) * P],
                                  hid[:, i % 2, :], start=(e == 0), stop=(e == NE - 1))
                    last.then_inc(f_down, 1)

                for i in range(NH * NE):
                    half, e = divmod(i, NE)
                    cols = slice(half * HALF, (half + 1) * HALF)
                    if i == 1:
                        pe.wait_ge(r_comb, b + 1)
                        for tt in range(NT):
                            last = nc.tensor.transpose(ps[0:E, 6 + tt // 4, (tt % 4) * P:(tt % 4 + 1) * P],
                                                       route[:, 5, tt * E:(tt + 1) * E], ident())
                        last.then_inc(cb_full, 1)
                        pe.wait_ge(cb_lo, b + 1)
                    if i >= 2:
                        pe.wait_ge(f_hid, b * NH * NE + i - 1)
                    bank = 2 + 3 * (i % 2)
                    for part in range(2):
                        last = split_mm(ps[:, bank + part, :], W_GU + (2 * e + part) * CT * HID, (HID, HID), cols)
                    if e:
                        last = mm(ps[:, bank + 2, :], wh[:, W_SEL + (e - 1) * P:W_SEL + e * P], comb_t[:, cols],
                                  start=True, stop=True)
                    last.then_inc(f_full, 1)
                    if i:
                        down(i - 1)
                down(NH * NE - 1)


def kernel(**inputs):
    import concourse.bacc as bacc
    from concourse.bass_utils import run_bass_kernel_spmd

    a = {k: np.asarray(v) for k, v in inputs.items()}

    def by_rows(w):
        return w.reshape(CT, P, -1).transpose(1, 0, 2).reshape(P, -1)

    def spread(vec):
        return np.broadcast_to(vec.reshape(1, -1), (P, vec.size))

    def column(vec):
        return vec.reshape(-1, P).T

    def pad(w):
        return np.concatenate([w, np.zeros((P - w.shape[0], w.shape[1]), np.float32)])

    L0, L1, L2 = "L0_conv_", "L1_attn_", "L1_ffn_"
    parts = [by_rows(a[L1 + n].T) for n in ("Q1_w", "K1_w", "Q2_w", "K2_w", "V_w", "out_w")]
    parts += [by_rows(a[L2 + "shared_gate"]), by_rows(a[L2 + "shared_up"])]
    for e in range(E):
        parts += [by_rows(a[L2 + "W_gate"][e]), by_rows(a[L2 + "W_up"][e])]
    parts.append(by_rows(a[L2 + "router"]))
    sel = np.zeros((P, E, P), np.float32)
    for e in range(E):
        sel[e, e] = sel[32 + e, e] = 0.5
    parts.append(sel.reshape(P, -1))
    w_split = np.ascontiguousarray(np.concatenate(parts, 1))

    qkv = np.concatenate([a[L0 + "Wq"].T, a[L0 + "Wk"].T, a[L0 + "Wv"].T], 1)
    group = np.arange(P) // 64
    blk = (group[:, None] == group[None, :]).astype(np.float32) / 256
    idx = np.tile(E - np.arange(E, dtype=np.float32), (P, NT))
    full = [by_rows(qkv), a[L2 + "shared_down"]] + [a[L2 + "W_down"][e] for e in range(E)]
    full += [pad(a[L0 + "Wo"].T), np.eye(P, dtype=np.float32), blk, idx]
    full += [np.tile(a[L0 + "bk"], 4)[:, None], pad(a[L0 + "bv"][:, None]), column(a[L0 + "bo"]),
             spread(a[L0 + "gamma"]), column(a[L1 + "K1_b"]), column(a[L1 + "K2_b"]), column(a[L1 + "gn_w"]),
             column(a[L1 + "gn_b"]), column(a[L1 + "out_b"])]
    full += [spread(a[L1 + "lambda_" + n]) for n in ("q1", "k1", "q2", "k2")] + [spread(a[L0 + "bq"])]
    w_full = np.ascontiguousarray(np.concatenate(full, 1))

    arrays = {"x_dram": np.ascontiguousarray(a["x"].reshape(B, C, N)), "w_split_dram": w_split,
              "w_full_dram": w_full}
    nc = bacc.Bacc("TRN2", target_bir_lowering=False, num_devices=1)
    args = [nc.dram_tensor(k, w.shape, mybir.dt.from_np(w.dtype), kind="ExternalInput").ap()
            for k, w in arrays.items()]
    out = nc.dram_tensor("y_dram", (B, C, N), F32, kind="ExternalOutput").ap()
    build(nc, *args, out)
    r = run_bass_kernel_spmd(nc, [arrays], core_ids=[0])
    return r.results[0]["y_dram"].reshape(B, C, 32, 32)
```

```python
from contextlib import ExitStack

import numpy as np

import concourse.bass as bass
from concourse import mybir

F32 = mybir.dt.float32
F32R = mybir.dt.float32r
ACT = mybir.ActivationFunctionType
ALU = mybir.AluOpType
AX = mybir.AxisListType

P = 128
B, C, N = 16, 256, 1024
CT = C // P
NT = N // P
HALF = 512
NH = N // HALF
CR = 32
NJ = N // CR // 4
HEADS, HD = 8, 32
UNITS = 2 * HEADS
SCALE = float(HD) ** -0.5
E, HID = 8, 128
NE = E + 1
CQ = 256
AUX = 96
KS = AUX + 2
NST, NP, NS = 4, 4, 2
PAIRS = NT // 2
LN_EPS = 1e-5

W_QK = 0
W_V = W_QK + 4 * CT * C
W_O = W_V + CT * C
W_R = W_O + CT * C
W_GU = W_R + CT * E
W_SEL = W_GU + NE * 2 * CT * HID
W_SPLIT = W_SEL + E
F_QKV = 0
F_DOWN = F_QKV + CT * 3 * CR
F_WO = F_DOWN + NE * C
F_ID = F_WO + C
F_BLK = F_ID + P
F_IDX = F_BLK + P
F_VEC = F_IDX + NT * E
(V_BK, V_BV, V_BO, V_GAM, V_K1B, V_K2B, V_GNW, V_GNB, V_OUTB, V_LAM, V_BQ) = (
    0, 1, 2, 4, 5, 7, 9, 11, 13, 15, 47)
F_ALL = F_VEC + V_BQ + CR

AHEAD = 2
PROJ_STEP = UNITS // 2 - 3


def ring_order():
    before = [("proj", t) for t in range(4)] + [("score", 0, q) for q in range(NT)] + [("turn", 0)]
    beside = {-1: before}
    for u in range(UNITS):
        beside[u] = [("proj", 4 + t) for t in range(4)] if u == PROJ_STEP else []
        items = [("score", u + AHEAD, q) for q in range(NT)] if u + AHEAD < UNITS else []
        if u >= 1 and u - 1 + AHEAD < UNITS:
            items.insert(1, ("turn", u - 1 + AHEAD))
        if u == 0:
            items = [("score", 1, q) for q in range(NT)] + items[:1] + [("turn", 1)] + items[1:]
        beside[u] += items
    return beside


BESIDE = ring_order()
RING = [item for u in range(-1, UNITS) for item in BESIDE[u]]
RING_AT = {item: n for n, item in enumerate(RING)}
SLOT_USES = [len(range(s, UNITS, NST)) for s in range(NST)]
STACK_DMAS, AUX_DMAS = 5, 2
DVE_STEPS = 141


def build(nc, x, w_split, w_full, out):
    ctx = ExitStack()
    with ctx:
        def sb(name, shape, dt=F32):
            return ctx.enter_context(nc.sbuf_tensor(name, shape, dt))

        def sem(name):
            return ctx.enter_context(nc.semaphore(name))

        wh = sb("w_hi", [P, W_SPLIT], F32R)
        wl = sb("w_lo", [P, W_SEL], F32R)
        wf = sb("w_full", [P, F_ALL])
        ones = sb("ones", [P, CR])
        gbo = sb("gamma_bo", [P, CT])
        nlam = sb("minus_lambda", [P, HEADS])
        xin = sb("x_tile", [P, CT, N])
        res = sb("residual", [P, CT, N])
        xh = sb("act_hi", [P, CT, N], F32R)
        xl = sb("act_lo", [P, CT, N], F32R)
        stage = sb("stage", [P, 2, 4, N])
        stack = sb("stack", [P, NST, 2, N], F32R)
        probs = sb("probs", [P, NP, N])
        psums = sb("prob_sums", [P, NS, N])
        vt = sb("v_tokens", [P, NT, C])
        ocm = xin
        oh = sb("o_head", [P, 2, CQ])
        rec = sb("recip_sum", [P, CQ])
        comb_t = stack[:, NST - 1, 0, :]
        nm = sb("minus_max", [P, 2, NT])
        mrow = sb("max_rows", [NT, 2, 2, P], F32R)
        small = sb("small", [P, 160])
        route = sb("route", [P, 6, NT * E])
        ot = route[:, 0:4, :].rearrange("p a n -> p (a n)")

        flat = stage[:, :, :, :].rearrange("p a t n -> p (a t n)")
        xt = flat[:, 0:NT * C].rearrange("p (t c) -> p t c", t=NT)
        qt_sb = flat[:, 2048:2048 + NJ * CR].rearrange("p (j c) -> p j c", j=NJ)
        k4_sb = flat[:, 2304:2304 + NJ * CR].rearrange("p (j c) -> p j c", j=NJ)
        a2_sb = flat[0:CR, 2560:2560 + C]
        at_sb = flat[0:CR, 2816:2816 + 5 * CR].rearrange("p (a c) -> p a c", a=5)
        v_sb = flat[0:CR, 3072:3072 + N]
        on_sb = flat[:, 0:CT * N].rearrange("p (t n) -> p t n", t=CT)
        th = flat[:, 0:2 * HALF].rearrange("p (s n) -> p s n", s=2)
        hid = flat[:, 1024:1024 + 2 * HALF].rearrange("p (s n) -> p s n", s=2)
        gu = flat[:, 2048:2048 + HALF]
        guu = flat[:, 2560:2560 + HALF]
        lrow = flat[:, 3072:3072 + N]

        ps = ctx.enter_context(nc.psum_tensor("psum", [P, 8, HALF], F32))

        def wide(slot):
            return ps[:, 2 * slot:2 * slot + 2, :]

        def ident():
            return wf[:, F_ID:F_ID + P]

        def vec(c, n=1, rows=P):
            return wf[0:rows, F_VEC + c:F_VEC + c + n]

        raw_in, full_in, setup = sem("raw_weights_in"), sem("full_weights_in"), sem("setup_done")
        setup_step = sem("setup_step")
        filled = sem("constants_filled")
        x_in, x_used, y_out = sem("x_in"), sem("x_used"), sem("y_out")
        step = sem("dve_step")
        c_full, c_ready, c_max, c_exp = sem("conv_filled"), sem("conv_ready"), sem("conv_max"), sem("conv_exp")
        t_full, t_var, t_sd, t_rs = sem("tokens_filled"), sem("ln_var"), sem("ln_sd"), sem("ln_rstd")
        n_act, n_dve = sem("ln_normed_act"), sem("ln_normed_dve")
        back_full, back_hi, back_lo = sem("back_filled"), sem("back_hi"), sem("back_lo")
        v_full, v_ready = sem("v_filled"), sem("v_ready")
        ring_full, ring_free = sem("ring_filled"), sem("ring_free")
        proj_hi = sem("proj_hi")
        stack_in = [sem(f"stack_in{s}") for s in range(NST)]
        aux_in = [sem(f"aux_in{s}") for s in range(NST)]
        st_full, p_ready, pv_done = sem("st_filled"), sem("probs_ready"), sem("pv_done")
        pair_ready, ones_done = sem("pair_ready"), sem("ones_done")
        o_free, oh_ready = sem("o_free"), sem("o_head_ready")
        o_in = [sem(f"o_in{s}") for s in range(2)]
        g_stat, g_full, g_var, g_sd = sem("gn_stat"), sem("gn_filled"), sem("gn_var"), sem("gn_sd")
        on_ready, on_hi, on_lo = sem("on_ready"), sem("on_hi"), sem("on_lo")
        y1_full, y1_ready = sem("y1_filled"), sem("y1_ready")
        r_full, r_rows, r_z, r_exp, r_comb = sem("router_filled"), sem("router_rows"), sem("router_z"), sem("router_exp"), sem("combine_ready")
        cb_full, cb_hi, cb_lo = sem("combine_filled"), sem("combine_hi"), sem("combine_lo")
        f_full, f_th, f_hid, f_down, f_out = (
            sem("ffn_filled"), sem("ffn_tanh"), sem("ffn_hidden"), sem("ffn_down"), sem("ffn_out"))

        block = ctx.enter_context(nc.Block())

        @block.sync
        def _(sp):
            sp.dma_start(wf[:, :], w_full).then_inc(full_in, 16)
            sp.dma_start(flat[:, 0:W_SPLIT], w_split).then_inc(raw_in, 16)
            sp.dma_start(xin[:, :, :], x[0].rearrange("(t p) n -> p t n", p=P)).then_inc(x_in, 16)

            def batch(b, more):
                def load_stack(u):
                    if u in (0, 1):
                        sp.wait_ge(ring_free, b * len(RING) + RING_AT["proj", 2 * u + 1] + 1)
                    elif u == 8:
                        sp.wait_ge(ring_free, b * len(RING) + RING_AT["proj", 7] + 1)
                    elif u >= NST:
                        sp.wait_ge(pv_done, b * UNITS * NT + (u - NST + 1) * NT)
                    s, rows, m = u % NST, slice(HD * (u // 2 % 4), HD * (u // 2 % 4) + HD), u % 2
                    st = stack[:, s, :, :].bitcast(F32)
                    parts = ((st[0:HD, :, :], stage[rows, 0, 2 * m:2 * m + 2, :]),
                             (st[HD:2 * HD, 0, :], stage[rows, 1, 2 * m, :]),
                             (st[HD:2 * HD, 1, :], stage[rows, 0, 2 * m + 1, :]),
                             (st[2 * HD:3 * HD, 0, :], stage[rows, 0, 2 * m, :]),
                             (st[2 * HD:3 * HD, 1, :], stage[rows, 1, 2 * m + 1, :]))
                    for dst, src in parts:
                        sp.dma_start(dst, src).then_inc(stack_in[s], 16)

                def load_aux(u):
                    sp.wait_ge(ring_free, b * len(RING) + RING_AT["turn", u] + 1)
                    for part in range(2):
                        sp.dma_start(stack[AUX + part:AUX + part + 1, u % NST, 0, :].bitcast(F32)
                                     .rearrange("p (t n) -> p t n", t=NT),
                                     mrow[:, u % 2, part, :].bitcast(F32)).then_inc(aux_in[u % NST], 16)

                def save_head(h):
                    sp.wait_ge(oh_ready, b * HEADS + h + 1)
                    for c in range(4):
                        sp.dma_start(ocm[HD * (h % 4):HD * (h % 4) + HD, h // 4, c * CQ:(c + 1) * CQ],
                                     oh[HD * c:HD * c + HD, h % 2, :]).then_inc(o_in[h % 2], 16)

                for u in (0, 1, 2, 3):
                    load_stack(u)
                load_aux(0)
                load_aux(1)
                for u in range(UNITS):
                    if u >= 1 and u - 1 + AHEAD < UNITS:
                        load_aux(u - 1 + AHEAD)
                    if u % 2 == 0 and u:
                        save_head(u // 2 - 1)
                    if u + NST < UNITS:
                        load_stack(u + NST)
                save_head(HEADS - 1)
                if more:
                    sp.wait_ge(on_ready, b * CT + CT)
                    sp.dma_start(xin[:, :, :], x[b + 1].rearrange("(t p) n -> p t n", p=P)).then_inc(x_in, 16)
                for half in range(NH):
                    sp.wait_ge(f_out, b * NH * CT + NH * CT + CT * (half + 1))
                    cols = slice(half * HALF, (half + 1) * HALF)
                    sp.dma_start(out[b].rearrange("(t p) n -> p t n", p=P)[:, :, cols],
                                 res[:, :, cols]).then_inc(y_out, 16)

            with sp.Fori(0, B - 1) as b:
                batch(b, True)
            batch(B - 1, False)
            sp.wait_ge(y_out, (B + 1) * NH * 16)

        @block.gpsimd
        def _(pool):
            nc.gpsimd.memset(ones[:, :], 1.0).then_inc(filled, 1)
            pool.wait_ge(filled, 1)
            nc.gpsimd.memset(stack[AUX:P, :, :, :].bitcast(F32), 1.0).then_inc(filled, 1)
            with pool.Fori(0, B) as b:
                for n in range(UNITS * PAIRS):
                    pool.wait_ge(p_ready, b * 2 * UNITS * NT + 4 * (n + 1))
                    if n >= NS:
                        pool.wait_ge(ones_done, b * UNITS * PAIRS + n - NS + 1)
                    nc.gpsimd.tensor_tensor(psums[:, n % NS, :], probs[:, 2 * n % NP, :],
                                            probs[:, (2 * n + 1) % NP, :], ALU.add).then_inc(pair_ready, 1)

        @block.scalar
        def _(act):
            act.wait_ge(raw_in, 16)
            nc.scalar.activation(wh[:, :], flat[:, 0:W_SPLIT], ACT.Copy).then_inc(setup, 1)
            act.wait_ge(full_in, 16)
            act.wait_ge(setup_step, 2)
            nc.scalar.activation(small[:, 16:32], small[:, 0:16], ACT.Exp).then_inc(setup_step, 1)
            with act.Fori(0, B) as b:
                act.wait_ge(c_max, b + 1)
                nc.scalar.activation(at_sb[:, 0, :], ps[0:CR, 4, 0:CR], ACT.Exp, bias=small[0:CR, 32:33],
                                     accum_out=small[0:CR, 33:34]).then_inc(c_exp, 1)

                def layer_norm(i):
                    act.wait_ge(t_var, b * 2 + i + 1)
                    nc.scalar.activation(small[:, 64:72], small[:, 56:64], ACT.Sqrt).then_inc(t_sd, 1)
                    act.wait_ge(t_rs, b * 2 + i + 1)
                    for k in range(2):
                        for tt in (2 * k, 2 * k + 1):
                            last = nc.scalar.activation(
                                xt[:, tt, :], ps[:, 4 + k, (tt % 2) * C:(tt % 2 + 1) * C], ACT.Identity,
                                bias=small[:, 80 + tt:81 + tt], scale=small[:, 72 + tt:73 + tt])
                        last.then_inc(n_act, 1)
                    for k in range(4):
                        act.wait_ge(back_full, b * 8 + 4 * i + k + 1)
                        cols = slice((k % 2) * HALF, (k % 2 + 1) * HALF)
                        nc.scalar.activation(xh[:, k // 2, cols], ps[:, k, :], ACT.Copy).then_inc(back_hi, 1)

                layer_norm(0)
                def project(g):
                    for t in range(4):
                        n = RING_AT["proj", 4 * g + t]
                        act.wait_ge(ring_full, b * len(RING) + n + 1)
                        if g and t == 0:
                            for s in range(NST):
                                done = len(range(s, 8, NST))
                                act.wait_ge(stack_in[s], (b * SLOT_USES[s] + done) * STACK_DMAS * 16)
                        dst = stage[:, 0, t, :].bitcast(F32R)
                        src = wide(n % 2).rearrange("p h n -> p (h n)")
                        if t % 2 == 0:
                            ins = nc.scalar.activation(dst, src, ACT.Copy, scale=SCALE)
                        else:
                            ins = nc.scalar.activation(dst, src, ACT.Identity,
                                                       bias=vec((V_K1B, V_K2B)[t // 2] + g))
                        ins.then_inc(proj_hi, 1)

                project(0)
                for k in range(4):
                    act.wait_ge(v_full, b * 4 + k + 1)
                    nc.scalar.activation(vt[:, 2 * k:2 * k + 2, :],
                                         ps[:, 4 + k, :].rearrange("p (t c) -> p t c", t=2),
                                         ACT.Copy).then_inc(v_ready, 1)

                for u in range(UNITS):
                    if u == PROJ_STEP:
                        project(1)
                    for kt in range(NT):
                        k = u * NT + kt
                        if k >= NP:
                            act.wait_ge(pv_done, b * UNITS * NT + k - NP + 1)
                            if k % 2 == 0:
                                act.wait_ge(pair_ready, b * UNITS * PAIRS + (k - NP) // 2 + 1)
                        for half in range(2):
                            act.wait_ge(st_full, b * 2 * UNITS * NT + 2 * k + half + 1)
                            nc.scalar.activation(probs[:, k % NP, half * HALF:(half + 1) * HALF],
                                                 ps[:, 4 + half, :], ACT.Exp).then_inc(p_ready, 1)
                act.wait_ge(g_var, b + 1)
                nc.scalar.activation(small[:, 104:106], small[:, 102:104], ACT.Sqrt).then_inc(g_sd, 1)
                for t in range(CT):
                    act.wait_ge(on_ready, b * CT + t + 1)
                    nc.scalar.activation(xh[:, t, :], on_sb[:, t, :], ACT.Copy).then_inc(on_hi, 1)
                layer_norm(1)
                act.wait_ge(r_z, b + 1)
                nc.scalar.activation(route[:, 1, :], route[:, 0, :], ACT.Exp).then_inc(r_exp, 1)
                for i in range(NH * NE):
                    if i == 1:
                        act.wait_ge(cb_full, b + 1)
                        nc.scalar.activation(comb_t[0:E, :], ps[0:E, 6:8, :].rearrange("p h n -> p (h n)"),
                                             ACT.Copy).then_inc(cb_hi, 1)
                    act.wait_ge(f_full, b * NH * NE + i + 1)
                    if i >= 2:
                        act.wait_ge(f_hid, b * NH * NE + i - 1)
                    nc.scalar.activation(th[:, i % 2, :], ps[:, 2 + 3 * (i % 2), :], ACT.Tanh,
                                         scale=0.5).then_inc(f_th, 1)

        @block.vector
        def _(dve):
            v = nc.vector
            dve.wait_ge(full_in, 16)
            lam = wf[:, F_VEC + V_LAM:F_VEC + V_LAM + 32].rearrange("p (m a h) -> p m a h", m=2, a=2)
            for m in range(2):
                v.tensor_tensor(small[:, 8 * m:8 * m + 8], lam[:, m, 0, :], lam[:, m, 1, :],
                                ALU.mult).then_inc(setup_step, 1)
            v.tensor_scalar(gbo[:, :], vec(V_BO, 2), vec(V_GAM), None, ALU.mult).then_inc(setup, 1)
            dve.wait_ge(setup_step, 3)
            v.tensor_tensor(small[:, 40:48], small[:, 24:32], small[:, 16:24], ALU.subtract).then_inc(setup_step, 1)
            dve.wait_ge(setup_step, 4)
            v.tensor_scalar(nlam[:, :], small[:, 40:48], -0.2, None, ALU.add).then_inc(setup, 1)
            dve.wait_ge(setup, 3)
            v.tensor_tensor(wl[:, :], flat[:, 0:W_SEL], wh[:, 0:W_SEL], ALU.subtract).then_inc(setup, 1)
            dve.wait_ge(setup, 4)
            v.memset(small[:, 0:1], 0.0).then_inc(f_out, NH * CT)
            v.memset(small[:, 1:2], 0.0).then_inc(y_out, NH * 16)

            with dve.Fori(0, B) as b:
                taken = [0]

                def link(ins):
                    taken[0] += 1
                    ins.then_inc(step, 1)
                    dve.wait_ge(step, b * DVE_STEPS + taken[0])

                dve.wait_ge(c_full, b * 7 + 1)
                v.tensor_tensor(qt_sb, ps[:, 0, 0:NJ * CR].rearrange("p (j c) -> p j c", j=NJ),
                                vec(V_BQ, CR).unsqueeze(1).broadcast_to([P, NJ, CR]), ALU.add)
                v.tensor_scalar(k4_sb, ps[:, 1, 0:NJ * CR].rearrange("p (j c) -> p j c", j=NJ),
                                vec(V_BK), None, ALU.add)
                v.tensor_scalar(v_sb, ps[0:CR, 2:4, :].rearrange("p h n -> p (h n)"),
                                vec(V_BV, rows=CR), None, ALU.add).then_inc(c_ready, 1)
                dve.wait_ge(c_full, b * 7 + 2)
                v.tensor_reduce(small[0:CR, 32:33], ps[0:CR, 4, 0:CR], AX.X, ALU.max, negate=True).then_inc(c_max, 1)
                dve.wait_ge(c_exp, b + 1)
                link(v.reciprocal(small[0:CR, 34:35], small[0:CR, 33:34]))
                v.tensor_scalar(at_sb[:, 1:5, :], at_sb[:, 0:1, :].broadcast_to([CR, 4, CR]), small[0:CR, 34:35],
                                None, ALU.mult).then_inc(c_ready, 1)
                dve.wait_ge(c_full, b * 7 + 3)
                v.tensor_scalar(a2_sb, ps[0:CR, 5, 0:C], vec(V_GAM, rows=CR), None, ALU.mult).then_inc(c_ready, 1)
                dve.wait_ge(y_out, b * NH * 16 + NH * 16)
                for k in range(4):
                    t, cols = k // 2, slice((k % 2) * HALF, (k % 2 + 1) * HALF)
                    dve.wait_ge(c_full, b * 7 + 4 + k)
                    v.scalar_tensor_tensor(res[:, t, cols], ps[:, k, :], gbo[:, t:t + 1], xin[:, t, cols],
                                           ALU.add, ALU.add).then_inc(x_used, 1)

                def layer_norm(i):
                    for k in range(4):
                        dve.wait_ge(t_full, b * 8 + 4 * i + k + 1)
                        for tt in (2 * k, 2 * k + 1):
                            v.bn_stats(small[:, 112 + 6 * (tt % 8):118 + 6 * (tt % 8)],
                                       ps[:, 4 + k, (tt % 2) * C:(tt % 2 + 1) * C]).then_inc(step, 1)
                            taken[0] += 1
                    dve.wait_ge(step, b * DVE_STEPS + taken[0])
                    even, odd = small[:, 113:160:6], small[:, 116:160:6]
                    link(v.tensor_tensor(small[:, 40:48], even, odd, ALU.add))
                    v.tensor_tensor(small[:, 48:56], small[:, 114:160:6], small[:, 117:160:6],
                                    ALU.add).then_inc(step, 1)
                    taken[0] += 1
                    link(v.tensor_tensor(small[:, 88:96], even, odd, ALU.subtract))
                    link(v.scalar_tensor_tensor(small[:, 88:96], small[:, 88:96], 0.25, small[:, 88:96],
                                                ALU.mult, ALU.mult))
                    link(v.tensor_scalar(small[:, 48:56], small[:, 48:56], 1.0 / C, LN_EPS, ALU.mult, ALU.add))
                    v.tensor_tensor(small[:, 56:64], small[:, 48:56], small[:, 88:96], ALU.add).then_inc(t_var, 1)
                    dve.wait_ge(t_sd, b * 2 + i + 1)
                    link(v.reciprocal(small[:, 72:80], small[:, 64:72]))
                    v.scalar_tensor_tensor(small[:, 80:88], small[:, 40:48], -0.5, small[:, 72:80],
                                           ALU.mult, ALU.mult).then_inc(t_rs, 1)
                    dve.wait_ge(t_rs, b * 2 + i + 1)
                    for k in range(2, 4):
                        for tt in (2 * k, 2 * k + 1):
                            last = v.tensor_scalar(xt[:, tt, :], ps[:, 4 + k, (tt % 2) * C:(tt % 2 + 1) * C],
                                                   small[:, 72 + tt:73 + tt], small[:, 80 + tt:81 + tt],
                                                   ALU.mult, ALU.add)
                        last.then_inc(n_dve, 1)
                    for k in range(4):
                        cols = slice((k % 2) * HALF, (k % 2 + 1) * HALF)
                        dve.wait_ge(back_hi, b * 8 + 4 * i + k + 1)
                        v.tensor_tensor(xl[:, k // 2, cols], ps[:, k, :], xh[:, k // 2, cols],
                                        ALU.subtract).then_inc(back_lo, 1)

                layer_norm(0)

                def ring_step(item):
                    n = RING_AT[item]
                    dve.wait_ge(ring_full, b * len(RING) + n + 1)
                    flat_in = wide(n % 2).rearrange("p h n -> p (h n)")
                    if item[0] == "proj":
                        t = item[1] % 4
                        dve.wait_ge(proj_hi, b * 8 + item[1] + 1)
                        dst, hi = stage[:, 1, t, :].bitcast(F32R), stage[:, 0, t, :]
                        bias = vec((V_K1B, V_K2B)[t // 2] + item[1] // 4)
                        v.scalar_tensor_tensor(dst, flat_in, SCALE if t % 2 == 0 else bias, hi,
                                               ALU.mult if t % 2 == 0 else ALU.add,
                                               ALU.subtract).then_inc(ring_free, 1)
                    elif item[0] == "score":
                        _, u, q = item
                        v.tensor_reduce(nm[:, u % 2, q:q + 1], flat_in, AX.X, ALU.max,
                                        negate=True).then_inc(ring_free, 1)
                    else:
                        u = item[1]
                        if u >= 2:
                            s = (u - 2) % NST
                            dve.wait_ge(aux_in[s], (b * SLOT_USES[s] + (u - 2) // NST + 1) * AUX_DMAS * 16)
                        rows = ps[0:NT, 2 * (n % 2), 0:P]
                        link(v.tensor_copy(mrow[:, u % 2, 0, :], rows))
                        v.tensor_tensor(mrow[:, u % 2, 1, :], rows, mrow[:, u % 2, 0, :],
                                        ALU.subtract).then_inc(ring_free, 1)

                def sum_recips(u, part):
                    dve.wait_ge(ones_done, b * UNITS * PAIRS + (u + 1) * PAIRS)
                    if u and part == 0:
                        dve.wait_ge(o_free, b * UNITS + u)
                    cols = slice(part * CQ // 2, (part + 1) * CQ // 2)
                    taken[0] += 1
                    v.reciprocal(rec[:, cols], ps[:, 6 + u % 2, CQ + cols.start:CQ + cols.stop]).then_inc(step, 1)

                def head_out(u):
                    h, bank = u // 2, 6 + u % 2
                    dve.wait_ge(step, b * DVE_STEPS + taken[0])
                    if u % 2 == 0:
                        if h >= 2:
                            dve.wait_ge(o_in[h % 2], (b * (HEADS // 2) + h // 2) * 4 * 16)
                        v.tensor_tensor(oh[:, h % 2, :], ps[:, bank, 0:CQ], rec[:, :], ALU.mult).then_inc(o_free, 1)
                    else:
                        v.scalar_tensor_tensor(ot[:, :], ps[:, bank, 0:CQ], nlam[:, h:h + 1], rec[:, :],
                                               ALU.mult, ALU.mult).then_inc(o_free, 1)
                        dve.wait_ge(o_free, b * UNITS + u + 1)
                        v.tensor_tensor(oh[:, h % 2, :], oh[:, h % 2, :], ot[:, :], ALU.add).then_inc(oh_ready, 1)

                for item in BESIDE[-1]:
                    ring_step(item)
                for u in range(UNITS + 1):
                    items = list(BESIDE.get(u, []))
                    if u == PROJ_STEP:
                        for item in items[:4]:
                            ring_step(item)
                        items = items[4:]
                    if u == 0:
                        for item in items:
                            ring_step(item)
                        continue
                    for n in range(6):
                        if items:
                            ring_step(items.pop(0))
                        if 3 <= n < 5:
                            sum_recips(u - 1, n - 3)
                    head_out(u - 1)
                    for item in items:
                        ring_step(item)

                for s in range(2):
                    dve.wait_ge(o_in[s], (b + 1) * (HEADS // 2) * 4 * 16)
                for t in range(CT):
                    for half in range(NH):
                        v.bn_stats(small[:, 112 + 12 * t + 6 * half:118 + 12 * t + 6 * half],
                                   ocm[:, t, half * HALF:(half + 1) * HALF]).then_inc(step, 1)
                        taken[0] += 1
                dve.wait_ge(step, b * DVE_STEPS + taken[0])
                means = small[:, 113:136:3]
                g_mean, g_sq = small[:, 0:8], small[:, 8:16]
                v.tensor_copy(g_mean, means).then_inc(step, 1)
                taken[0] += 1
                link(v.tensor_tensor(small[:, 16:24], means, means, ALU.mult))
                link(v.scalar_tensor_tensor(g_sq, small[:, 114:136:3], 4.0 / N, small[:, 16:24],
                                            ALU.mult, ALU.add))
                v.tensor_reduce(small[:, 92:96], small[:, 0:16].rearrange("p (a n) -> p a n", n=4), AX.X,
                                ALU.add).then_inc(g_stat, 1)
                dve.wait_ge(g_full, b + 1)
                link(v.tensor_copy(small[:, 96:100], ps[:, 0, 0:4]))
                link(v.tensor_tensor(small[:, 100:102], small[:, 96:98], small[:, 96:98], ALU.mult))
                link(v.tensor_tensor(small[:, 100:102], small[:, 98:100], small[:, 100:102], ALU.subtract))
                v.tensor_scalar(small[:, 102:104], small[:, 100:102], LN_EPS, None, ALU.add).then_inc(g_var, 1)
                dve.wait_ge(g_sd, b + 1)
                link(v.reciprocal(small[:, 106:108], small[:, 104:106]))
                link(v.tensor_tensor(small[:, 106:108], small[:, 106:108], vec(V_GNW, 2), ALU.mult))
                link(v.tensor_tensor(small[:, 108:110], small[:, 96:98], small[:, 106:108], ALU.mult))
                link(v.tensor_tensor(small[:, 108:110], vec(V_GNB, 2), small[:, 108:110], ALU.subtract))
                for t in range(CT):
                    v.tensor_scalar(on_sb[:, t, :], ocm[:, t, :], small[:, 106 + t:107 + t],
                                    small[:, 108 + t:109 + t], ALU.mult, ALU.add).then_inc(on_ready, 1)
                for t in range(CT):
                    dve.wait_ge(on_hi, b * CT + t + 1)
                    v.tensor_tensor(xl[:, t, :], on_sb[:, t, :], xh[:, t, :], ALU.subtract).then_inc(on_lo, 1)
                for k in range(4):
                    t, cols = k // 2, slice((k % 2) * HALF, (k % 2 + 1) * HALF)
                    dve.wait_ge(y1_full, b * 4 + k + 1)
                    v.scalar_tensor_tensor(res[:, t, cols], ps[:, k, :], vec(V_OUTB + t), res[:, t, cols],
                                           ALU.add, ALU.add).then_inc(y1_ready, 1)
                layer_norm(1)

                def r3(i):
                    return route[:, i, :].rearrange("p (t e) -> p t e", t=NT)

                def wide8(col):
                    return small[:, col:col + NT].unsqueeze(2).broadcast_to([P, NT, E])

                dve.wait_ge(r_full, b * 2 + 1)
                v.tensor_copy(lrow, ps[:, 0:2, :].rearrange("p h n -> p (h n)")).then_inc(r_rows, 1)
                dve.wait_ge(r_full, b * 2 + 2)
                lg = ps[:, 0, 0:NT * E].rearrange("p (t e) -> p t e", t=NT)
                link(v.tensor_reduce(small[:, 0:8], lg, AX.X, ALU.max, negate=True))
                v.tensor_tensor(r3(0), lg, wide8(0), ALU.add).then_inc(r_z, 1)
                dve.wait_ge(r_exp, b + 1)
                link(v.tensor_reduce(small[:, 0:8], r3(1), AX.X, ALU.add))
                link(v.reciprocal(small[:, 8:16], small[:, 0:8]))
                link(v.tensor_tensor(r3(0), r3(1), wide8(8), ALU.mult))
                idx = wf[:, F_IDX:F_IDX + NT * E].rearrange("p (t e) -> p t e", t=NT)
                source = 0
                for rank in range(2):
                    link(v.tensor_reduce(small[:, 0:8], r3(source), AX.X, ALU.max))
                    link(v.tensor_tensor(r3(1), r3(source), wide8(0), ALU.is_equal))
                    link(v.tensor_tensor(r3(1), r3(1), idx, ALU.mult))
                    link(v.tensor_reduce(small[:, 8:16], r3(1), AX.X, ALU.max))
                    link(v.tensor_tensor(r3(2 + rank), r3(1), wide8(8), ALU.is_equal))
                    if rank == 0:
                        link(v.scalar_tensor_tensor(r3(4), r3(2), -2.0, r3(0), ALU.mult, ALU.add))
                        source = 4
                link(v.tensor_tensor(r3(2), r3(2), r3(3), ALU.add))
                v.tensor_tensor(r3(5), r3(2), r3(0), ALU.mult).then_inc(r_comb, 1)

                for i in range(NH * NE):
                    half, e = divmod(i, NE)
                    if i == 1:
                        dve.wait_ge(cb_hi, b + 1)
                        v.tensor_tensor(comb_t[32:32 + E, :], ps[0:E, 6:8, :].rearrange("p h n -> p (h n)"),
                                        comb_t[0:E, :], ALU.subtract).then_inc(cb_lo, 1)
                    bank = 2 + 3 * (i % 2)
                    dve.wait_ge(f_th, b * NH * NE + i + 1)
                    if i:
                        dve.wait_ge(f_hid, b * NH * NE + i)
                    link(v.scalar_tensor_tensor(gu, th[:, i % 2, :], 1.0, ps[:, bank, :], ALU.add, ALU.mult))
                    if i >= 2:
                        dve.wait_ge(f_down, b * NH * NE + i - 1)
                    if e == 0:
                        v.scalar_tensor_tensor(hid[:, i % 2, :], gu, 0.5, ps[:, bank + 1, :],
                                               ALU.mult, ALU.mult).then_inc(f_hid, 1)
                    else:
                        link(v.tensor_tensor(guu, gu, ps[:, bank + 1, :], ALU.mult))
                        v.tensor_tensor(hid[:, i % 2, :], guu, ps[:, bank + 2, :], ALU.mult).then_inc(f_hid, 1)
                    if e == NE - 1:
                        dve.wait_ge(f_down, b * NH * NE + i + 1)
                        for t in range(CT):
                            cols = slice(half * HALF, (half + 1) * HALF)
                            v.tensor_tensor(res[:, t, cols], ps[:, t, :], res[:, t, cols],
                                            ALU.add).then_inc(f_out, 1)
                assert taken[0] == DVE_STEPS, taken[0]

        @block.tensor
        def _(pe):
            mm = nc.tensor.matmul

            def split_mm(dst, w, wn, act_cols, first=True, last=True):
                n, ins = 0, None
                for kt in range(CT):
                    for wt, xx in ((wh, xh), (wl, xh), (wh, xl)):
                        ins = mm(dst, wt[:, w + kt * wn[0]:w + kt * wn[0] + wn[1]], xx[:, kt, act_cols],
                                 start=(first and n == 0), stop=(last and n == 3 * CT - 1))
                        n += 1
                return ins

            pe.wait_ge(full_in, 16)
            pe.wait_ge(setup, 4)
            pe.wait_ge(filled, 2)
            with pe.Fori(0, B) as b:
                pe.wait_ge(x_in, b * 16 + 16)
                pe.wait_ge(f_out, b * NH * CT + NH * CT)
                xq = xin[:, :, :].rearrange("p t (c j q) -> p t j q c", c=CR, j=NJ)
                xk = xin[:, :, :].rearrange("p t (j q d) -> p t q j d", q=4, d=CR)
                wq = wf[:, F_QKV:F_QKV + CT * 3 * CR].rearrange("p (t w c) -> p t w c", t=CT, w=3)
                for j in range(NJ):
                    for kt in range(CT):
                        for q in range(4):
                            mm(ps[CR * q:CR * q + CR, 0, j * CR:(j + 1) * CR], xq[:, kt, j, q, :], wq[:, kt, 0, :],
                               start=(kt == 0), stop=(kt == CT - 1))
                for q in range(4):
                    for kt in range(CT):
                        mm(ps[CR * q:CR * q + CR, 1, 0:NJ * CR], wq[:, kt, 1, :], xk[:, kt, q, :, :],
                           start=(kt == 0), stop=(kt == CT - 1))
                for half in range(NH):
                    for kt in range(CT):
                        last = mm(ps[0:CR, 2 + half, :], wq[:, kt, 2, :],
                                  xin[:, kt, half * HALF:(half + 1) * HALF], start=(kt == 0), stop=(kt == CT - 1))
                last.then_inc(c_full, 1)
                pe.wait_ge(c_ready, b * 3 + 1)
                for j in range(NJ):
                    last = mm(ps[0:CR, 4, 0:CR], qt_sb[:, j, :], k4_sb[:, j, :], start=(j == 0), stop=(j == NJ - 1))
                last.then_inc(c_full, 1)
                pe.wait_ge(c_ready, b * 3 + 2)
                mm(ps[:, 5, 0:C], at_sb[:, 1:5, :].rearrange("p a c -> p (a c)"), wf[0:CR, F_WO:F_WO + C], start=True, stop=True).then_inc(c_full, 1)
                pe.wait_ge(c_ready, b * 3 + 3)
                for k in range(4):
                    mm(ps[:, k, :], a2_sb[:, (k // 2) * P:(k // 2 + 1) * P], v_sb[:, (k % 2) * HALF:(k % 2 + 1) * HALF],
                       start=True, stop=True).then_inc(c_full, 1)

                def layer_norm(i):
                    if i == 0:
                        pe.wait_ge(x_used, b * 4 + 4)
                    else:
                        pe.wait_ge(y1_ready, b * 4 + 4)
                    for tt in range(NT):
                        for ct in range(CT):
                            last = nc.tensor.transpose(ps[:, 4 + tt // 2, (tt % 2) * C + ct * P:(tt % 2) * C + ct * P + P],
                                                       res[:, ct, tt * P:(tt + 1) * P], ident())
                        if tt % 2:
                            last.then_inc(t_full, 1)
                    pe.wait_ge(n_act, b * 4 + 2 * i + 2)
                    pe.wait_ge(n_dve, b * 4 + 2 * i + 2)
                    for k in range(4):
                        for q in range(4):
                            tt = 4 * (k % 2) + q
                            last = nc.tensor.transpose(ps[:, k, q * P:(q + 1) * P],
                                                       xt[:, tt, (k // 2) * P:(k // 2 + 1) * P], ident())
                        last.then_inc(back_full, 1)
                    pe.wait_ge(back_lo, b * 8 + 4 * i + 4)

                layer_norm(0)
                def ring_step(item):
                    n = RING_AT[item]
                    if n >= 2:
                        pe.wait_ge(ring_free, b * len(RING) + n - 1)
                    slot = wide(n % 2)
                    if item[0] == "proj":
                        g, t = divmod(item[1], 4)
                        for half in range(NH):
                            last = split_mm(slot[:, half, :], W_QK + t * CT * C + g * P, (C, P),
                                            slice(half * HALF, (half + 1) * HALF))
                    elif item[0] == "score":
                        _, u, q = item
                        s = u % NST
                        if q == 0:
                            pe.wait_ge(stack_in[s], (b * SLOT_USES[s] + u // NST + 1) * STACK_DMAS * 16)
                        for half in range(NH):
                            last = mm(slot[:, half, :], stack[0:AUX, s, 0, q * P:(q + 1) * P],
                                      stack[0:AUX, s, 1, half * HALF:(half + 1) * HALF], start=True, stop=True)
                    else:
                        u = item[1]
                        pe.wait_ge(ring_free, b * len(RING) + RING_AT["score", u, NT - 1] + 1)
                        last = nc.tensor.transpose(slot[0:NT, 0, 0:P], nm[:, u % 2, :], ident())
                    last.then_inc(ring_full, 1)

                def weighted(u, kt):
                    h, k, bank = u // 2, u * NT + kt, 6 + u % 2
                    pe.wait_ge(p_ready, b * 2 * UNITS * NT + 2 * k + 2)
                    if kt == 0 and u >= 2:
                        pe.wait_ge(o_free, b * UNITS + u - 1)
                    for c in range(4):
                        last = mm(ps[HD * c:HD * c + HD, bank, 0:CQ], vt[:, kt, HD * h:HD * h + HD],
                                  probs[:, k % NP, c * CQ:(c + 1) * CQ], start=(kt == 0),
                                  stop=(kt == NT - 1), skip_group_check=True)
                    last.then_inc(pv_done, 1)

                def add_up(n):
                    u, pair = divmod(n, PAIRS)
                    pe.wait_ge(pair_ready, b * UNITS * PAIRS + n + 1)
                    for c in range(4):
                        last = mm(ps[HD * c:HD * c + HD, 6 + u % 2, CQ:2 * CQ], ones[:, :],
                                  psums[:, n % NS, c * CQ:(c + 1) * CQ], start=False,
                                  stop=(pair == PAIRS - 1), skip_group_check=True)
                    last.then_inc(ones_done, 1)

                for item in BESIDE[-1][:4]:
                    ring_step(item)
                for tt in range(NT):
                    n = 0
                    for kt in range(CT):
                        for xx, wt in ((xh, wh), (xh, wl), (xl, wh)):
                            last = mm(ps[:, 4 + tt // 2, (tt % 2) * C:(tt % 2 + 1) * C], xx[:, kt, tt * P:(tt + 1) * P],
                                      wt[:, W_V + kt * C:W_V + (kt + 1) * C], start=(n == 0), stop=(n == 5))
                            n += 1
                    if tt % 2:
                        last.then_inc(v_full, 1)
                for item in BESIDE[-1][4:]:
                    ring_step(item)
                pe.wait_ge(v_ready, b * 4 + 4)
                for u in range(UNITS):
                    items = list(BESIDE[u])
                    if u == PROJ_STEP:
                        for item in items[:4]:
                            ring_step(item)
                        items = items[4:]
                    s = u % NST
                    pe.wait_ge(aux_in[s], (b * SLOT_USES[s] + u // NST + 1) * AUX_DMAS * 16)
                    for kt in range(NT):
                        k = u * NT + kt
                        for half in range(NH):
                            if k >= 1:
                                pe.wait_ge(p_ready, b * 2 * UNITS * NT + 2 * k + half - 1)
                            mm(ps[:, 4 + half, :], stack[0:KS, s, 1, kt * P:(kt + 1) * P],
                               stack[0:KS, s, 0, half * HALF:(half + 1) * HALF], start=True,
                               stop=True).then_inc(st_full, 1)
                        for _ in range((2 if kt == 1 else 1) + (u == 0)):
                            if items:
                                ring_step(items.pop(0))
                        if k >= 1:
                            weighted(*divmod(k - 1, NT))
                        if k >= 3 and k % 2:
                            add_up((k - 3) // 2)
                    assert not items
                weighted(UNITS - 1, NT - 1)
                add_up(UNITS * PAIRS - 1)

                pe.wait_ge(g_stat, b + 1)
                mm(ps[:, 0, 0:4], wf[:, F_BLK:F_BLK + P], small[:, 92:96], start=True, stop=True).then_inc(g_full, 1)
                pe.wait_ge(on_lo, b * CT + CT)
                for k in range(4):
                    split_mm(ps[:, k, :], W_O + (k // 2) * P, (C, P),
                             slice((k % 2) * HALF, (k % 2 + 1) * HALF)).then_inc(y1_full, 1)
                layer_norm(1)

                for half in range(NH):
                    last = split_mm(ps[:, half, :], W_R, (E, P), slice(half * HALF, (half + 1) * HALF))
                last.then_inc(r_full, 1)
                pe.wait_ge(r_rows, b + 1)
                nc.tensor.transpose(ps[:, 0, 0:P], lrow[:, 0:P], ident())
                for tt in range(1, NT):
                    last = nc.tensor.transpose(ps[:, 0, tt * E:(tt + 1) * E], lrow[0:E, tt * P:(tt + 1) * P],
                                               wf[0:E, F_ID:F_ID + E])
                last.then_inc(r_full, 1)

                def down(i):
                    half, e = divmod(i, NE)
                    pe.wait_ge(f_hid, b * NH * NE + i + 1)
                    if e == 0 and half:
                        pe.wait_ge(f_out, b * NH * CT + NH * CT + CT * half)
                    for t in range(CT):
                        last = mm(ps[:, t, :], wf[:, F_DOWN + e * C + t * P:F_DOWN + e * C + (t + 1) * P],
                                  hid[:, i % 2, :], start=(e == 0), stop=(e == NE - 1))
                    last.then_inc(f_down, 1)

                for i in range(NH * NE):
                    half, e = divmod(i, NE)
                    cols = slice(half * HALF, (half + 1) * HALF)
                    if i == 1:
                        pe.wait_ge(r_comb, b + 1)
                        for tt in range(NT):
                            last = nc.tensor.transpose(ps[0:E, 6 + tt // 4, (tt % 4) * P:(tt % 4 + 1) * P],
                                                       route[:, 5, tt * E:(tt + 1) * E], ident())
                        last.then_inc(cb_full, 1)
                        pe.wait_ge(cb_lo, b + 1)
                    if i >= 2:
                        pe.wait_ge(f_hid, b * NH * NE + i - 1)
                    bank = 2 + 3 * (i % 2)
                    for part in range(2):
                        last = split_mm(ps[:, bank + part, :], W_GU + (2 * e + part) * CT * HID, (HID, HID), cols)
                    if e:
                        last = mm(ps[:, bank + 2, :], wh[:, W_SEL + e - 1:W_SEL + e].broadcast_to([P, P]), comb_t[:, cols],
                                  start=True, stop=True)
                    last.then_inc(f_full, 1)
                    if i:
                        down(i - 1)
                down(NH * NE - 1)


def kernel(**inputs):
    import concourse.bacc as bacc
    from concourse.bass_utils import run_bass_kernel_spmd

    a = {k: np.asarray(v) for k, v in inputs.items()}

    def by_rows(w):
        return w.reshape(CT, P, -1).transpose(1, 0, 2).reshape(P, -1)

    def spread(vec):
        return np.broadcast_to(vec.reshape(1, -1), (P, vec.size))

    def column(vec):
        return vec.reshape(-1, P).T

    def pad(w):
        return np.concatenate([w, np.zeros((P - w.shape[0], w.shape[1]), np.float32)])

    L0, L1, L2 = "L0_conv_", "L1_attn_", "L1_ffn_"
    parts = [by_rows(a[L1 + n].T) for n in ("Q1_w", "K1_w", "Q2_w", "K2_w", "V_w", "out_w")]
    parts.append(by_rows(a[L2 + "router"]))
    parts += [by_rows(a[L2 + "shared_gate"]), by_rows(a[L2 + "shared_up"])]
    for e in range(E):
        parts += [by_rows(a[L2 + "W_gate"][e]), by_rows(a[L2 + "W_up"][e])]
    sel = np.zeros((P, E), np.float32)
    for e in range(E):
        sel[e, e] = sel[32 + e, e] = 0.5
    parts.append(sel)
    w_split = np.ascontiguousarray(np.concatenate(parts, 1))

    qkv = np.concatenate([a[L0 + "Wq"].T, a[L0 + "Wk"].T, a[L0 + "Wv"].T], 1)
    group = np.arange(P) // 64
    blk = (group[:, None] == group[None, :]).astype(np.float32) / 256
    idx = np.tile(E - np.arange(E, dtype=np.float32), (P, NT))
    full = [by_rows(qkv), a[L2 + "shared_down"]] + [a[L2 + "W_down"][e] for e in range(E)]
    full += [pad(a[L0 + "Wo"].T), np.eye(P, dtype=np.float32), blk, idx]
    full += [np.tile(a[L0 + "bk"], 4)[:, None], pad(a[L0 + "bv"][:, None]), column(a[L0 + "bo"]),
             spread(a[L0 + "gamma"]), column(a[L1 + "K1_b"]), column(a[L1 + "K2_b"]), column(a[L1 + "gn_w"]),
             column(a[L1 + "gn_b"]), column(a[L1 + "out_b"])]
    full += [spread(a[L1 + "lambda_" + n]) for n in ("q1", "k1", "q2", "k2")] + [spread(a[L0 + "bq"])]
    w_full = np.ascontiguousarray(np.concatenate(full, 1))

    arrays = {"x_dram": np.ascontiguousarray(a["x"].reshape(B, C, N)), "w_split_dram": w_split,
              "w_full_dram": w_full}
    nc = bacc.Bacc("TRN2", target_bir_lowering=False, num_devices=1)
    args = [nc.dram_tensor(k, w.shape, mybir.dt.from_np(w.dtype), kind="ExternalInput").ap()
            for k, w in arrays.items()]
    out = nc.dram_tensor("y_dram", (B, C, N), F32, kind="ExternalOutput").ap()
    build(nc, *args, out)
    r = run_bass_kernel_spmd(nc, [arrays], core_ids=[0])
    return r.results[0]["y_dram"].reshape(B, C, 32, 32)
```

```python
from contextlib import ExitStack

import numpy as np

import concourse.bass as bass
from concourse import mybir

F32 = mybir.dt.float32
F32R = mybir.dt.float32r
ACT = mybir.ActivationFunctionType
ALU = mybir.AluOpType
AX = mybir.AxisListType

P = 128
B, C, N = 16, 256, 1024
CT = C // P
NT = N // P
HALF = 512
NH = N // HALF
CR = 32
NR = N // P
HEADS, HD = 8, 32
UNITS = 2 * HEADS
SCALE = float(HD) ** -0.5
E, HID = 8, 128
NE = E + 1
CQ = 256
AUX = 96
KS = AUX + 2
NST, NP, NS = 3, 4, 2
QUAD = 4
QUADS = NT // QUAD
SHARE = 64
ADDED = UNITS * NT - 2
LN_EPS = 1e-5

W_QK = 0
W_V = W_QK + 4 * CT * C
W_O = W_V + CT * C
W_R = W_O + CT * C
W_GU = W_R + CT * E
W_DOWN = W_GU + NE * 2 * CT * HID
W_SEL = W_DOWN + NE * C
W_SPLIT = W_SEL + E
F_QKV = 0
F_WO = F_QKV + CT * 3 * CR
F_ID = F_WO + C
F_BLK = F_ID + P
F_IDX = F_BLK + P
F_VEC = F_IDX + NT * E
(V_BVK, V_BO, V_GAM, V_K1B, V_K2B, V_GNW, V_GNB, V_OUTB, V_LAM, V_BQ) = (
    0, 1, 3, 4, 6, 8, 10, 12, 14, 46)
F_ALL = F_VEC + V_BQ + CR

def adds(tile):
    return (QUAD - 1) * (tile // QUAD) + max(tile % QUAD, 1)


ADDS = adds(ADDED - 1)
ADD_AT = QUAD + 3


AHEAD = NT + 4
PROJ_BESIDE = ((5, 3), (5, 5), (5, 7), (6, 1))


def back_bank(i, k):
    return k if i else (k + 2) % 4


def ring_order():
    before = [("proj", t) for t in range(4)] + [("score", 0, q) for q in range(NT)] + [("turn", 0)]
    before += [("score", *divmod(n, NT)) for n in range(NT, AHEAD)]
    beside = {}
    for u in range(UNITS):
        for kt in range(NT):
            beside[u, kt] = [("turn", u + 1)] if kt == 2 * NT - AHEAD and u + 1 < UNITS else []
            n = u * NT + kt + AHEAD
            if n < UNITS * NT:
                beside[u, kt].append(("score", *divmod(n, NT)))
            if (u, kt) in PROJ_BESIDE:
                beside[u, kt].append(("proj", 4 + PROJ_BESIDE.index((u, kt))))
    return before, beside


BEFORE, BESIDE = ring_order()
RING = BEFORE + [item for place in sorted(BESIDE) for item in BESIDE[place]]
RING_AT = {item: n for n, item in enumerate(RING)}
SLOT_USES = [len(range(s, UNITS, NST)) for s in range(NST)]
STACK_DMAS, AUX_DMAS = 5, 2
DVE_STEPS = 144
FIRST_STEPS = 14


def build(nc, x, w_split, w_full, out):
    ctx = ExitStack()
    with ctx:
        def sb(name, shape, dt=F32):
            return ctx.enter_context(nc.sbuf_tensor(name, shape, dt))

        def sem(name):
            return ctx.enter_context(nc.semaphore(name))

        wh = sb("w_hi", [P, W_SPLIT], F32R)
        wl = sb("w_lo", [P, W_SEL], F32R)
        wf = sb("w_full", [P, F_ALL])
        ones = sb("ones", [P, CR])
        gbo = sb("gamma_bo", [P, CT])
        nlam = sb("minus_lambda", [P, HEADS])
        xin = sb("x_tile", [P, CT, N])
        res = sb("residual", [P, CT, N])
        xh = sb("act_hi", [P, CT, N], F32R)
        xl = sb("act_lo", [P, CT, N], F32R)
        stage = sb("stage", [P, 2, 4, N])
        stack = sb("stack", [P, NST, 2, N], F32R)
        probs = sb("probs", [P, NP, N])
        psums = sb("prob_sums", [P, NS, N])
        vt = sb("v_tokens", [P, NT, C])
        ocm = xin
        oh = sb("o_head", [P, 2, CQ])
        rec = sb("recip_sum", [P, CQ])
        comb_t = stack[:, NST - 1, 0, :]
        nm = sb("minus_max", [P, 2, NT])
        mrow = sb("max_rows", [NT, 2, P], F32R)
        small = sb("small", [P, 160])

        route = sb("route", [P, 6, NT * E])
        ot = route[:, 0:4, :].rearrange("p a n -> p (a n)")

        flat = stage[:, :, :, :].rearrange("p a t n -> p (a t n)")
        xt = flat[:, 0:NT * C].rearrange("p (t c) -> p t c", t=NT)
        vk_sb = flat[0:2 * CR, 4096:4096 + N]
        qt_sb = flat[:, 5120:5120 + NR * CR].rearrange("p (r c) -> p r c", r=NR)
        kt_sb = flat[:, 5376:5376 + NR * CR].rearrange("p (r c) -> p r c", r=NR)
        a2_sb = flat[0:CR, 5632:5632 + C]
        at_sb = flat[0:CR, 5888:5888 + 5 * CR].rearrange("p (a c) -> p a c", a=5)
        on_sb = flat[:, 0:CT * N].rearrange("p (t n) -> p t n", t=CT)
        raw_rest = probs[:, :, :].rearrange("p s n -> p (s n)")[:, 0:W_SPLIT - W_DOWN]
        th = flat[:, 0:2 * HALF].rearrange("p (s n) -> p s n", s=2)
        hid = flat[:, 1024:1024 + 2 * HALF].rearrange("p (s n) -> p s n", s=2)
        hh, hl = (stack[:, slot, 0, :].rearrange("p (s n) -> p s n", s=2) for slot in range(2))
        gu = flat[:, 2048:2048 + HALF]
        guu = flat[:, 2560:2560 + HALF]
        lrow = flat[:, 3072:3072 + N]
        last_out = flat[:, 3072:3072 + CT * HALF].rearrange("p (t n) -> p t n", t=CT)

        ps = ctx.enter_context(nc.psum_tensor("psum", [P, 8, HALF], F32))

        def wide(slot):
            return ps[:, 2 - 2 * slot:4 - 2 * slot, :]

        def ident():
            return wf[:, F_ID:F_ID + P]

        def vec(c, n=1, rows=P):
            return wf[0:rows, F_VEC + c:F_VEC + c + n]

        def conv_small(c):
            return small[0:CR, 32 + c:33 + c]

        raw_in, full_in, setup = sem("raw_weights_in"), sem("full_weights_in"), sem("setup_done")
        setup_step = sem("setup_step")
        filled = sem("constants_filled")
        x_in, x_used, res_saved = sem("x_in"), sem("x_used"), sem("residual_saved")
        y_out = [sem(f"y_out{half}") for half in range(NH)]
        step = sem("dve_step")
        q_full, q_ready = sem("conv_q_filled"), sem("conv_q_ready")
        vk_full, vk_ready = sem("conv_vk_filled"), sem("conv_vk_ready")
        kt_in, a_full, a_max, a_exp = sem("conv_keys_in"), sem("conv_scores_filled"), sem("conv_max"), sem("conv_exp")
        a_rec, a_ready = sem("conv_recip"), sem("conv_probs_ready")
        a2_full, a2_ready = sem("conv_wo_filled"), sem("conv_wo_ready")
        c_full = sem("conv_filled")
        t_full, t_var, t_sd, t_rs = sem("tokens_filled"), sem("ln_var"), sem("ln_sd"), sem("ln_rstd")
        n_act, n_dve = sem("ln_normed_act"), sem("ln_normed_dve")
        back_full, back_hi, back_lo = sem("back_filled"), sem("back_hi"), sem("back_lo")
        v_full, v_ready = sem("v_filled"), sem("v_ready")
        ring_full, ring_free = sem("ring_filled"), sem("ring_free")
        proj_hi = sem("proj_hi")
        stack_in = [sem(f"stack_in{s}") for s in range(NST)]
        aux_in = [sem(f"aux_in{s}") for s in range(NST)]
        st_full, p_ready, pv_done = sem("st_filled"), sem("probs_ready"), sem("pv_done")
        sum_pool, sum_dve, ones_done = sem("sum_by_pool"), sem("sum_by_dve"), sem("ones_done")
        o_free, oh_ready = sem("o_free"), sem("o_head_ready")
        o_in = [sem(f"o_in{s}") for s in range(2)]
        g_stat, g_full, g_var, g_sd = sem("gn_stat"), sem("gn_filled"), sem("gn_var"), sem("gn_sd")
        g_coef = sem("gn_coefficients")
        on_ready, on_hi, on_lo = sem("on_ready"), sem("on_hi"), sem("on_lo")
        y1_full, y1_ready = sem("y1_filled"), sem("y1_ready")
        r_full, r_rows, r_z, r_exp = sem("router_filled"), sem("router_rows"), sem("router_z"), sem("router_exp")
        r_comb = sem("combine_ready")
        cb_full, cb_hi, cb_lo = sem("combine_filled"), sem("combine_hi"), sem("combine_lo")
        f_full, f_th, f_hid, f_hi, f_lo, f_down, f_out = (
            sem("ffn_filled"), sem("ffn_tanh"), sem("ffn_hidden"), sem("ffn_hidden_hi"), sem("ffn_hidden_lo"), sem("ffn_down"), sem("ffn_out"))

        def add_tile(engine, queue, b, k, cols, made):
            n, j = divmod(k, QUAD)
            total = psums[:, n % NS, cols]
            queue.wait_ge(p_ready, b * 2 * UNITS * NT + 2 * k + 2)
            if j == 1 and n >= NS:
                queue.wait_ge(ones_done, b * UNITS * QUADS + n - NS + 1)
            if j > 1:
                queue.wait_ge(made, b * ADDS + adds(k) - 1)
            engine.tensor_tensor(total, total if j > 1 else probs[:, (k - 1) % NP, cols], probs[:, k % NP, cols],
                                 ALU.add).then_inc(made, 1)

        block = ctx.enter_context(nc.Block())

        @block.sync
        def _(sp):
            sp.dma_start(wf[:, :], w_full).then_inc(full_in, 16)
            sp.dma_start(flat[:, 0:W_DOWN], w_split[:, 0:W_DOWN]).then_inc(raw_in, 16)
            sp.dma_start(raw_rest, w_split[:, W_DOWN:W_SPLIT]).then_inc(raw_in, 16)
            sp.dma_start(xin[:, :, :], x[0].rearrange("(t p) n -> p t n", p=P)).then_inc(x_in, 16)

            def load_keys(n):
                sp.wait_ge(vk_ready, n * NH + NH)
                sp.dma_start(kt_sb.rearrange("p r c -> p (r c)"), vk_sb[CR:2 * CR, :]
                             .rearrange("p (a n) -> p a n", a=4)).then_inc(kt_in, 16)

            load_keys(0)

            def batch(b, following):
                def load_stack(u):
                    s, rows, m = u % NST, slice(HD * (u // 2 % 4), HD * (u // 2 % 4) + HD), u % 2
                    st = stack[:, s, :, :].bitcast(F32)
                    q_parts = ((st[HD:2 * HD, 0, :], stage[rows, 1, 2 * m, :]),
                               (st[2 * HD:3 * HD, 0, :], stage[rows, 0, 2 * m, :]))
                    k_parts = ((st[0:HD, :, :], stage[rows, 0, 2 * m:2 * m + 2, :]),
                               (st[HD:2 * HD, 1, :], stage[rows, 0, 2 * m + 1, :]),
                               (st[2 * HD:3 * HD, 1, :], stage[rows, 1, 2 * m + 1, :]))
                    for t, parts in ((2 * m, q_parts), (2 * m + 1, k_parts)):
                        if u < 2:
                            sp.wait_ge(ring_free, b * len(RING) + RING_AT["proj", t] + 1)
                        elif u >= NST and t == 2 * m:
                            sp.wait_ge(pv_done, b * UNITS * NT + (u - NST + 1) * NT)
                        for dst, src in parts:
                            sp.dma_start(dst, src).then_inc(stack_in[s], 16)

                def load_aux(u):
                    sp.wait_ge(ring_free, b * len(RING) + RING_AT["turn", u] + 1)
                    for part in range(2):
                        sp.dma_start(stack[AUX + part:AUX + part + 1, u % NST, 0, :].bitcast(F32)
                                     .rearrange("p (t n) -> p t n", t=NT),
                                     mrow[:, part, :].bitcast(F32)).then_inc(aux_in[u % NST], 16)

                def save_head(h):
                    sp.wait_ge(oh_ready, b * HEADS + h + 1)
                    for c in range(4):
                        sp.dma_start(ocm[HD * (h % 4):HD * (h % 4) + HD, h // 4, c * CQ:(c + 1) * CQ],
                                     oh[HD * c:HD * c + HD, h % 2, :]).then_inc(o_in[h % 2], 16)

                for u in range(NST):
                    load_stack(u)
                load_aux(0)
                for u in range(UNITS):
                    if u and u - 1 + NST < UNITS:
                        load_stack(u - 1 + NST)
                    if u + 1 < UNITS:
                        load_aux(u + 1)
                    if u % 2 == 0 and u:
                        save_head(u // 2 - 1)
                save_head(HEADS - 1)
                sp.wait_ge(on_lo, b * NH * CT + NH * CT)
                sp.dma_start(xin[:, :, :], x[following].rearrange("(t p) n -> p t n", p=P)).then_inc(x_in, 16)
                load_keys(b + 1)
                for half in range(NH):
                    sp.wait_ge(f_out, b * NH * CT + CT + CT * (half + 1))
                    cols = slice(half * HALF, (half + 1) * HALF)
                    sp.dma_start(out[b].rearrange("(t p) n -> p t n", p=P)[:, :, cols],
                                 last_out if half else res[:, :, cols]).then_inc(y_out[half], 16)

            with sp.Fori(0, B - 1) as b:
                batch(b, b + 1)
            batch(B - 1, B - 1)
            sp.wait_ge(y_out[0], B * 16)
            sp.wait_ge(y_out[1], (B + 1) * 16)

        @block.gpsimd
        def _(pool):
            nc.gpsimd.memset(ones[:, :], 1.0).then_inc(filled, 1)
            pool.wait_ge(filled, 1)
            nc.gpsimd.memset(stack[AUX:P, :, :, :].bitcast(F32), 1.0).then_inc(filled, 1)
            with pool.Fori(0, B) as b:
                for k in range(ADDED):
                    if k % QUAD:
                        add_tile(nc.gpsimd, pool, b, k, slice(0, N - SHARE), sum_pool)

        @block.scalar
        def _(act):
            act.wait_ge(raw_in, 32)
            nc.scalar.activation(wh[:, 0:W_DOWN], flat[:, 0:W_DOWN], ACT.Copy).then_inc(setup, 1)
            nc.scalar.activation(wh[:, W_DOWN:W_SPLIT], raw_rest, ACT.Copy).then_inc(setup, 1)
            act.wait_ge(full_in, 16)
            act.wait_ge(setup_step, 2)
            nc.scalar.activation(small[:, 16:32], small[:, 0:16], ACT.Exp).then_inc(setup_step, 1)

            def conv_vk(n, half):
                act.wait_ge(vk_full, n * NH + half + 1)
                nc.scalar.activation(vk_sb[:, half * HALF:(half + 1) * HALF], ps[0:2 * CR, 2 + 2 * half, :],
                                     ACT.Identity, bias=vec(V_BVK, rows=2 * CR)).then_inc(vk_ready, 1)

            def conv_exp(n):
                act.wait_ge(a_max, n + 1)
                nc.scalar.activation(at_sb[:, 0, :], ps[0:CR, 7, 0:CR], ACT.Exp, bias=conv_small(0),
                                     accum_out=conv_small(1)).then_inc(a_exp, 1)

            act.wait_ge(setup, 6)
            conv_vk(0, 0)
            conv_vk(0, 1)
            conv_exp(0)

            def normalise(n, i):
                act.wait_ge(t_var, n * 2 + i + 1)
                nc.scalar.activation(small[:, 64:72], small[:, 56:64], ACT.Sqrt).then_inc(t_sd, 1)
                act.wait_ge(t_rs, n * 2 + i + 1)
                for k in range(2):
                    for tt in (2 * k, 2 * k + 1):
                        last = nc.scalar.activation(
                            xt[:, tt, :], ps[:, 6 + k, (tt % 2) * C:(tt % 2 + 1) * C], ACT.Identity,
                            bias=small[:, 80 + tt:81 + tt], scale=small[:, 72 + tt:73 + tt])
                    last.then_inc(n_act, 1)

            normalise(0, 0)
            with act.Fori(0, B) as b:
                def layer_norm(i):
                    if i == 1:
                        conv_vk(b + 1, 0)
                    for k in range(4):
                        act.wait_ge(back_full, b * 8 + 4 * i + k + 1)
                        cols = slice((k // 2) * HALF, (k // 2 + 1) * HALF)
                        nc.scalar.activation(xh[:, k % 2, cols], ps[:, back_bank(i, k), :], ACT.Copy).then_inc(back_hi, 1)

                layer_norm(0)
                def project(n):
                    g, t = divmod(n, 4)
                    act.wait_ge(ring_full, b * len(RING) + RING_AT["proj", n] + 1)
                    dst = stage[:, 0, t, :].bitcast(F32R)
                    src = wide(RING_AT["proj", n] % 2).rearrange("p h n -> p (h n)")
                    if t % 2 == 0:
                        ins = nc.scalar.activation(dst, src, ACT.Copy, scale=SCALE)
                    else:
                        ins = nc.scalar.activation(dst, src, ACT.Identity,
                                                   bias=vec((V_K1B, V_K2B)[t // 2] + g))
                    ins.then_inc(proj_hi, 1)

                act.wait_ge(y_out[1], b * 16 + 16)
                for t in range(4):
                    project(t)
                for k in range(4):
                    act.wait_ge(v_full, b * 4 + k + 1)
                    nc.scalar.activation(vt[:, 2 * k:2 * k + 2, :],
                                         ps[:, 4 + k, :].rearrange("p (t c) -> p t c", t=2),
                                         ACT.Copy).then_inc(v_ready, 1)

                for u in range(UNITS):
                    for kt in range(NT):
                        k = u * NT + kt
                        if k >= NP:
                            act.wait_ge(pv_done, b * UNITS * NT + k - NP + 1)
                            if k % QUAD != 1:
                                act.wait_ge(sum_pool, b * ADDS + adds(k - NP))
                                act.wait_ge(sum_dve, b * ADDS + adds(k - NP))
                        for half in range(2):
                            act.wait_ge(st_full, b * 2 * UNITS * NT + 2 * k + half + 1)
                            nc.scalar.activation(probs[:, k % NP, half * HALF:(half + 1) * HALF],
                                                 ps[:, 4 + half, :], ACT.Exp).then_inc(p_ready, 1)
                        for item in BESIDE[u, kt]:
                            if item[0] == "proj":
                                if item[1] == 4:
                                    for s in range(NST):
                                        done = len(range(s, 8, NST))
                                        act.wait_ge(stack_in[s], (b * SLOT_USES[s] + done) * STACK_DMAS * 16)
                                project(item[1])
                act.wait_ge(g_var, b + 1)
                nc.scalar.activation(small[:, 104:106], small[:, 102:104], ACT.Sqrt).then_inc(g_sd, 1)
                act.wait_ge(g_coef, b + 1)
                for s in range(2):
                    act.wait_ge(o_in[s], (b + 1) * (HEADS // 2) * 4 * 16)
                for half in range(NH):
                    cols = slice(half * HALF, (half + 1) * HALF)
                    for t in range(CT):
                        nc.scalar.activation(xh[:, t, cols], ocm[:, t, cols], ACT.Identity, scale=small[:, 106 + t:107 + t],
                                             bias=small[:, 108 + t:109 + t]).then_inc(on_hi, 1)
                normalise(b, 1)
                layer_norm(1)
                act.wait_ge(r_z, b + 1)
                nc.scalar.activation(route[:, 1, :], route[:, 0, :], ACT.Exp).then_inc(r_exp, 1)
                def hidden_hi(i):
                    act.wait_ge(f_hid, b * NH * NE + i + 1)
                    if i >= 2:
                        act.wait_ge(f_down, b * NH * NE + i - 1)
                    nc.scalar.activation(hh[:, i % 2, :], hid[:, i % 2, :], ACT.Copy).then_inc(f_hi, 1)

                for i in range(NH * NE):
                    if i == 3:
                        nc.scalar.activation(last_out, res[:, :, HALF:N], ACT.Copy).then_inc(res_saved, 1)
                    if i == 1:
                        act.wait_ge(cb_full, b + 1)
                        nc.scalar.activation(comb_t[0:E, :], ps[0:E, 0:2, :].rearrange("p h n -> p (h n)"),
                                             ACT.Copy).then_inc(cb_hi, 1)
                        conv_vk(b + 1, 1)
                    if i == NE + 1:
                        conv_exp(b + 1)
                    act.wait_ge(f_full, b * NH * NE + i + 1)
                    if i >= 2:
                        act.wait_ge(f_hid, b * NH * NE + i - 1)
                    nc.scalar.activation(th[:, i % 2, :], ps[:, 2 + 3 * (i % 2), :], ACT.Tanh,
                                         scale=0.5).then_inc(f_th, 1)
                    if i:
                        hidden_hi(i - 1)
                hidden_hi(NH * NE - 1)
                normalise(b + 1, 0)

        @block.vector
        def _(dve):
            v = nc.vector
            dve.wait_ge(full_in, 16)
            lam = wf[:, F_VEC + V_LAM:F_VEC + V_LAM + 32].rearrange("p (m a h) -> p m a h", m=2, a=2)
            for m in range(2):
                v.tensor_tensor(small[:, 8 * m:8 * m + 8], lam[:, m, 0, :], lam[:, m, 1, :],
                                ALU.mult).then_inc(setup_step, 1)
            v.tensor_scalar(gbo[:, :], vec(V_BO, 2), vec(V_GAM), None, ALU.mult).then_inc(setup, 1)
            dve.wait_ge(setup_step, 3)
            v.tensor_tensor(small[:, 40:48], small[:, 24:32], small[:, 16:24], ALU.subtract).then_inc(setup_step, 1)
            dve.wait_ge(setup_step, 4)
            v.tensor_scalar(nlam[:, :], small[:, 40:48], -0.2, None, ALU.add).then_inc(setup, 1)
            dve.wait_ge(setup, 4)
            v.tensor_tensor(wl[:, 0:W_DOWN], flat[:, 0:W_DOWN], wh[:, 0:W_DOWN], ALU.subtract).then_inc(setup, 1)
            v.tensor_tensor(wl[:, W_DOWN:W_SEL], raw_rest[:, 0:W_SEL - W_DOWN], wh[:, W_DOWN:W_SEL],
                            ALU.subtract).then_inc(setup, 1)
            dve.wait_ge(setup, 6)
            v.memset(small[:, 1:2], 0.0).then_inc(f_out, CT)
            v.memset(small[:, 0:1], 0.0).then_inc(y_out[1], 16)


            def conv_q(n):
                dve.wait_ge(q_full, n + 1)
                v.tensor_tensor(qt_sb, ps[:, 1, 0:NR * CR].rearrange("p (r c) -> p r c", r=NR),
                                vec(V_BQ, CR).unsqueeze(1).broadcast_to([P, NR, CR]), ALU.add).then_inc(q_ready, 1)

            def conv_max(n):
                dve.wait_ge(a_full, n + 1)
                v.tensor_reduce(conv_small(0), ps[0:CR, 7, 0:CR], AX.X, ALU.max, negate=True).then_inc(a_max, 1)

            def conv_probs(n):
                dve.wait_ge(a_exp, n + 1)
                v.reciprocal(conv_small(2), conv_small(1)).then_inc(a_rec, 1)
                dve.wait_ge(a_rec, n + 1)
                v.tensor_scalar(at_sb[:, 1:5, :], at_sb[:, 0:1, :].broadcast_to([CR, 4, CR]), conv_small(2),
                                None, ALU.mult).then_inc(a_ready, 1)

            def conv_wo(n):
                dve.wait_ge(a2_full, n + 1)
                v.tensor_scalar(a2_sb, ps[0:CR, 7, 0:C], vec(V_GAM, rows=CR), None, ALU.mult).then_inc(a2_ready, 1)

            def residual(n, half):
                cols = slice(half * HALF, (half + 1) * HALF)
                for t in range(CT):
                    k = CT * half + t
                    dve.wait_ge(c_full, n * 4 + 1 + k)
                    v.scalar_tensor_tensor(res[:, t, cols], ps[:, 2 + k, :], gbo[:, t:t + 1], xin[:, t, cols],
                                           ALU.add, ALU.add).then_inc(x_used, 1)

            conv_q(0)
            conv_max(0)
            conv_probs(0)
            conv_wo(0)
            for half in range(NH):
                residual(0, half)
            taken = [0]

            def link_from(base, ins):
                taken[0] += 1
                ins.then_inc(step, 1)
                dve.wait_ge(step, base + taken[0])

            def statistics(n, i, base):
                for k in range(4):
                    dve.wait_ge(t_full, n * 8 + 4 * i + k + 1)
                    for tt in (2 * k, 2 * k + 1):
                        v.bn_stats(small[:, 112 + 6 * (tt % 8):118 + 6 * (tt % 8)],
                                   ps[:, 4 + (k + 2) % 4, (tt % 2) * C:(tt % 2 + 1) * C]).then_inc(step, 1)
                        taken[0] += 1
                dve.wait_ge(step, base + taken[0])
                even, odd = small[:, 113:160:6], small[:, 116:160:6]
                link_from(base, v.tensor_tensor(small[:, 40:48], even, odd, ALU.add))
                v.tensor_tensor(small[:, 48:56], small[:, 114:160:6], small[:, 117:160:6],
                                ALU.add).then_inc(step, 1)
                taken[0] += 1
                link_from(base, v.tensor_tensor(small[:, 88:96], even, odd, ALU.subtract))
                link_from(base, v.scalar_tensor_tensor(small[:, 88:96], small[:, 88:96], 0.25, small[:, 88:96],
                                            ALU.mult, ALU.mult))
                link_from(base, v.tensor_scalar(small[:, 48:56], small[:, 48:56], 1.0 / C, LN_EPS, ALU.mult, ALU.add))
                v.tensor_tensor(small[:, 56:64], small[:, 48:56], small[:, 88:96], ALU.add).then_inc(t_var, 1)

            def normalise(n, i, base):
                dve.wait_ge(t_sd, n * 2 + i + 1)
                link_from(base, v.reciprocal(small[:, 72:80], small[:, 64:72]))
                v.scalar_tensor_tensor(small[:, 80:88], small[:, 40:48], -0.5, small[:, 72:80],
                                       ALU.mult, ALU.mult).then_inc(t_rs, 1)
                dve.wait_ge(t_rs, n * 2 + i + 1)
                for k in range(2, 4):
                    for tt in (2 * k, 2 * k + 1):
                        last = v.tensor_scalar(xt[:, tt, :], ps[:, 2 + k, (tt % 2) * C:(tt % 2 + 1) * C],
                                               small[:, 72 + tt:73 + tt], small[:, 80 + tt:81 + tt],
                                               ALU.mult, ALU.add)
                    last.then_inc(n_dve, 1)

            statistics(0, 0, 0)
            normalise(0, 0, 0)
            assert taken[0] == FIRST_STEPS, taken[0]
            with dve.Fori(0, B) as b:
                taken[0] = 0
                base = b * DVE_STEPS + FIRST_STEPS

                def link(ins):
                    link_from(base, ins)

                def layer_norm(i):
                    if i == 1:
                        conv_q(b + 1)
                    for k in range(4):
                        cols = slice((k // 2) * HALF, (k // 2 + 1) * HALF)
                        dve.wait_ge(back_hi, b * 8 + 4 * i + k + 1)
                        v.tensor_tensor(xl[:, k % 2, cols], ps[:, back_bank(i, k), :], xh[:, k % 2, cols],
                                        ALU.subtract).then_inc(back_lo, 1)

                layer_norm(0)

                def ring_step(item):
                    n = RING_AT[item]
                    dve.wait_ge(ring_full, b * len(RING) + n + 1)
                    flat_in = wide(n % 2).rearrange("p h n -> p (h n)")
                    if item[0] == "proj":
                        t = item[1] % 4
                        dve.wait_ge(proj_hi, b * 8 + item[1] + 1)
                        dst, hi = stage[:, 1, t, :].bitcast(F32R), stage[:, 0, t, :]
                        bias = vec((V_K1B, V_K2B)[t // 2] + item[1] // 4)
                        v.scalar_tensor_tensor(dst, flat_in, SCALE if t % 2 == 0 else bias, hi,
                                               ALU.mult if t % 2 == 0 else ALU.add,
                                               ALU.subtract).then_inc(ring_free, 1)
                    elif item[0] == "score":
                        _, u, q = item
                        v.tensor_reduce(nm[:, u % 2, q:q + 1], flat_in, AX.X, ALU.max,
                                        negate=True).then_inc(ring_free, 1)
                    else:
                        u = item[1]
                        if u:
                            s = (u - 1) % NST
                            dve.wait_ge(aux_in[s], (b * SLOT_USES[s] + (u - 1) // NST + 1) * AUX_DMAS * 16)
                        rows = wide(n % 2)[0:NT, 0, 0:P]
                        link(v.tensor_copy(mrow[:, 0, :], rows))
                        v.tensor_tensor(mrow[:, 1, :], rows, mrow[:, 0, :],
                                        ALU.subtract).then_inc(ring_free, 1)

                def sum_recips(u, part):
                    dve.wait_ge(ones_done, b * UNITS * QUADS + (u + 1) * QUADS)
                    if u and part == 0:
                        dve.wait_ge(o_free, b * UNITS + u)
                    cols = slice(part * CQ // 2, (part + 1) * CQ // 2)
                    taken[0] += 1
                    v.reciprocal(rec[:, cols], ps[:, 6 + u % 2, CQ + cols.start:CQ + cols.stop]).then_inc(step, 1)

                def head_out(u):
                    h, bank = u // 2, 6 + u % 2
                    dve.wait_ge(step, base + taken[0])
                    if u % 2 == 0:
                        if h >= 2:
                            dve.wait_ge(o_in[h % 2], (b * (HEADS // 2) + h // 2) * 4 * 16)
                        v.tensor_tensor(oh[:, h % 2, :], ps[:, bank, 0:CQ], rec[:, :], ALU.mult).then_inc(o_free, 1)
                    else:
                        v.scalar_tensor_tensor(ot[:, :], ps[:, bank, 0:CQ], nlam[:, h:h + 1], rec[:, :],
                                               ALU.mult, ALU.mult).then_inc(o_free, 1)
                        dve.wait_ge(o_free, b * UNITS + u + 1)
                        v.tensor_tensor(oh[:, h % 2, :], oh[:, h % 2, :], ot[:, :], ALU.add).then_inc(oh_ready, 1)
                        dve.wait_ge(oh_ready, b * HEADS + h + 1)
                        v.bn_stats(small[:, 112 + 6 * h:118 + 6 * h], oh[:, h % 2, :]).then_inc(step, 1)
                        taken[0] += 1

                for item in BEFORE:
                    ring_step(item)
                for u in range(UNITS + 1):
                    for kt in range(NT):
                        for item in BESIDE.get((u, kt), []):
                            ring_step(item)
                        k = u * NT + kt - 1
                        if 0 <= k < ADDED and k % QUAD:
                            add_tile(v, dve, b, k, slice(N - SHARE, N), sum_dve)
                        if u and kt in (3, 4):
                            sum_recips(u - 1, kt - 3)
                        if u and kt == 5:
                            head_out(u - 1)

                dve.wait_ge(step, base + taken[0])
                means = small[:, 113:160:3]
                v.tensor_copy(small[:, 0:16], means).then_inc(step, 1)
                taken[0] += 1
                link(v.tensor_tensor(small[:, 40:56], means, means, ALU.mult))
                link(v.scalar_tensor_tensor(small[:, 16:32], small[:, 114:160:3], 2.0 / CQ, small[:, 40:56],
                                            ALU.mult, ALU.add))
                v.tensor_reduce(small[:, 88:96], small[:, 0:32].rearrange("p (a n) -> p a n", n=4), AX.X,
                                ALU.add).then_inc(g_stat, 1)
                dve.wait_ge(g_full, b + 1)
                groups = ps[:, 0, 0:8].rearrange("p (a s) -> p a s", s=2)
                for side in range(2):
                    rows = slice(64 * side, 64 * side + 64)
                    v.tensor_copy(small[rows, 96:100], groups[rows, :, side]).then_inc(step, 1)
                    taken[0] += 1
                dve.wait_ge(step, base + taken[0])
                link(v.tensor_tensor(small[:, 100:102], small[:, 96:98], small[:, 96:98], ALU.mult))
                link(v.tensor_tensor(small[:, 100:102], small[:, 98:100], small[:, 100:102], ALU.subtract))
                v.tensor_scalar(small[:, 102:104], small[:, 100:102], LN_EPS, None, ALU.add).then_inc(g_var, 1)
                dve.wait_ge(g_sd, b + 1)
                link(v.reciprocal(small[:, 106:108], small[:, 104:106]))
                link(v.tensor_tensor(small[:, 106:108], small[:, 106:108], vec(V_GNW, 2), ALU.mult))
                link(v.tensor_tensor(small[:, 108:110], small[:, 96:98], small[:, 106:108], ALU.mult))
                v.tensor_tensor(small[:, 108:110], vec(V_GNB, 2), small[:, 108:110], ALU.subtract).then_inc(g_coef, 1)
                dve.wait_ge(g_coef, b + 1)
                for s in range(2):
                    dve.wait_ge(o_in[s], (b + 1) * (HEADS // 2) * 4 * 16)
                for half in range(NH):
                    cols = slice(half * HALF, (half + 1) * HALF)
                    for t in range(CT):
                        v.tensor_scalar(on_sb[:, t, cols], ocm[:, t, cols], small[:, 106 + t:107 + t],
                                        small[:, 108 + t:109 + t], ALU.mult, ALU.add).then_inc(on_ready, 1)
                    for t in range(CT):
                        dve.wait_ge(on_ready, b * NH * CT + half * CT + t + 1)
                        dve.wait_ge(on_hi, b * NH * CT + half * CT + t + 1)
                        v.tensor_tensor(xl[:, t, cols], on_sb[:, t, cols], xh[:, t, cols],
                                        ALU.subtract).then_inc(on_lo, 1)
                for k in range(4):
                    t, cols = k % 2, slice((k // 2) * HALF, (k // 2 + 1) * HALF)
                    dve.wait_ge(y1_full, b * 4 + k + 1)
                    v.scalar_tensor_tensor(res[:, t, cols], ps[:, k, :], vec(V_OUTB + t), res[:, t, cols],
                                           ALU.add, ALU.add).then_inc(y1_ready, 1)
                statistics(b, 1, base)
                normalise(b, 1, base)
                layer_norm(1)

                def r3(i):
                    return route[:, i, :].rearrange("p (t e) -> p t e", t=NT)

                def wide8(col):
                    return small[:, col:col + NT].unsqueeze(2).broadcast_to([P, NT, E])

                dve.wait_ge(r_full, b * 2 + 1)
                v.tensor_copy(lrow, ps[:, 0:2, :].rearrange("p h n -> p (h n)")).then_inc(r_rows, 1)
                dve.wait_ge(r_full, b * 2 + 2)
                lg = ps[:, 0, 0:NT * E].rearrange("p (t e) -> p t e", t=NT)
                link(v.tensor_reduce(small[:, 0:8], lg, AX.X, ALU.max, negate=True))
                v.tensor_tensor(r3(0), lg, wide8(0), ALU.add).then_inc(r_z, 1)
                dve.wait_ge(r_exp, b + 1)
                link(v.tensor_reduce(small[:, 0:8], r3(1), AX.X, ALU.add))
                link(v.reciprocal(small[:, 8:16], small[:, 0:8]))
                link(v.tensor_tensor(r3(0), r3(1), wide8(8), ALU.mult))
                idx = wf[:, F_IDX:F_IDX + NT * E].rearrange("p (t e) -> p t e", t=NT)
                source = 0
                for rank in range(2):
                    link(v.tensor_reduce(small[:, 0:8], r3(source), AX.X, ALU.max))
                    link(v.tensor_tensor(r3(1), r3(source), wide8(0), ALU.is_equal))
                    link(v.tensor_tensor(r3(1), r3(1), idx, ALU.mult))
                    link(v.tensor_reduce(small[:, 8:16], r3(1), AX.X, ALU.max))
                    link(v.tensor_tensor(r3(2 + rank), r3(1), wide8(8), ALU.is_equal))
                    if rank == 0:
                        link(v.scalar_tensor_tensor(r3(4), r3(2), -2.0, r3(0), ALU.mult, ALU.add))
                        source = 4
                link(v.tensor_tensor(r3(2), r3(2), r3(3), ALU.add))
                v.tensor_tensor(r3(5), r3(2), r3(0), ALU.mult).then_inc(r_comb, 1)

                def hidden_lo(i):
                    dve.wait_ge(f_hi, b * NH * NE + i + 1)
                    v.tensor_tensor(hl[:, i % 2, :], hid[:, i % 2, :], hh[:, i % 2, :], ALU.subtract).then_inc(f_lo, 1)

                def sum_out(half):
                    dve.wait_ge(f_down, b * NH * NE + (half + 1) * NE)
                    for t in range(CT):
                        cols = slice(half * HALF, (half + 1) * HALF)
                        onto = last_out[:, t, :] if half else res[:, t, cols]
                        v.tensor_tensor(onto, ps[:, t, :], onto, ALU.add).then_inc(f_out, 1)

                for i in range(NH * NE):
                    half, e = divmod(i, NE)
                    if i == 1:
                        dve.wait_ge(cb_hi, b + 1)
                        v.tensor_tensor(comb_t[32:32 + E, :], ps[0:E, 0:2, :].rearrange("p h n -> p (h n)"),
                                        comb_t[0:E, :], ALU.subtract).then_inc(cb_lo, 1)
                    if i == NE + 1:
                        conv_max(b + 1)
                        conv_probs(b + 1)
                    if i == NE + 2:
                        conv_wo(b + 1)
                    bank = 2 + 3 * (i % 2)
                    dve.wait_ge(f_th, b * NH * NE + i + 1)
                    if i:
                        dve.wait_ge(f_hid, b * NH * NE + i)
                    link(v.scalar_tensor_tensor(gu, th[:, i % 2, :], 1.0, ps[:, bank, :], ALU.add, ALU.mult))
                    if i >= 2:
                        dve.wait_ge(f_lo, b * NH * NE + i - 1)
                    if e == 0:
                        v.scalar_tensor_tensor(hid[:, i % 2, :], gu, 0.5, ps[:, bank + 1, :],
                                               ALU.mult, ALU.mult).then_inc(f_hid, 1)
                    else:
                        link(v.tensor_tensor(guu, gu, ps[:, bank + 1, :], ALU.mult))
                        v.tensor_tensor(hid[:, i % 2, :], guu, ps[:, bank + 2, :], ALU.mult).then_inc(f_hid, 1)
                    if i:
                        hidden_lo(i - 1)
                    if i == NE + 1:
                        sum_out(0)
                dve.wait_ge(y_out[0], b * 16 + 16)
                residual(b + 1, 0)
                dve.wait_ge(res_saved, b + 1)
                residual(b + 1, 1)
                hidden_lo(NH * NE - 1)
                statistics(b + 1, 0, base)
                normalise(b + 1, 0, base)
                sum_out(1)
                assert taken[0] == DVE_STEPS, taken[0]

        @block.tensor
        def _(pe):
            mm = nc.tensor.matmul

            def split_mm(dst, w, wn, act_cols, first=True, last=True):
                n, ins = 0, None
                for kt in range(CT):
                    for wt, xx in ((wh, xh), (wl, xh), (wh, xl)):
                        ins = mm(dst, wt[:, w + kt * wn[0]:w + kt * wn[0] + wn[1]], xx[:, kt, act_cols],
                                 start=(first and n == 0), stop=(last and n == 3 * CT - 1))
                        n += 1
                return ins

            pe.wait_ge(full_in, 16)
            pe.wait_ge(setup, 6)
            pe.wait_ge(filled, 2)

            wqvk = wf[:, F_QKV:F_QKV + CT * 3 * CR].rearrange("p (t w) -> p t w", t=CT)

            def conv_q(n):
                pe.wait_ge(x_in, n * 16 + 16)
                xq = xin[:, :, :].rearrange("p t (m r) -> p t r m", r=NR)
                for r in range(NR):
                    for kt in range(CT):
                        last = mm(ps[:, 1, r * CR:(r + 1) * CR], xq[:, kt, r, :], wqvk[:, kt, 0:CR],
                                  start=(kt == 0), stop=(kt == CT - 1))
                last.then_inc(q_full, 1)

            def conv_vk(half):
                for kt in range(CT):
                    last = mm(ps[0:2 * CR, 2 + 2 * half, :], wqvk[:, kt, CR:3 * CR],
                              xin[:, kt, half * HALF:(half + 1) * HALF], start=(kt == 0), stop=(kt == CT - 1))
                last.then_inc(vk_full, 1)

            def conv_scores(n):
                pe.wait_ge(q_ready, n + 1)
                pe.wait_ge(kt_in, n * 16 + 16)
                for r in range(NR):
                    last = mm(ps[0:CR, 7, 0:CR], qt_sb[:, r, :], kt_sb[:, r, :], start=(r == 0), stop=(r == NR - 1))
                last.then_inc(a_full, 1)

            def conv_wo(n):
                pe.wait_ge(a_ready, n + 1)
                mm(ps[:, 7, 0:C], at_sb[:, 1:5, :].rearrange("p a c -> p (a c)"), wf[0:CR, F_WO:F_WO + C],
                   start=True, stop=True).then_inc(a2_full, 1)

            def conv_last(k):
                mm(ps[:, 2 + k, :], a2_sb[:, (k % 2) * P:(k % 2 + 1) * P],
                   vk_sb[0:CR, (k // 2) * HALF:(k // 2 + 1) * HALF], start=True, stop=True).then_inc(c_full, 1)

            conv_q(0)
            for half in range(NH):
                conv_vk(half)
            conv_scores(0)
            conv_wo(0)
            pe.wait_ge(a2_ready, 1)
            for k in range(4):
                conv_last(k)

            def tokens(n, i):
                for tt in range(NT):
                    if tt % 4 == 0:
                        pe.wait_ge((x_used, y1_ready)[i], n * 4 + tt // 2 + 2)
                    for ct in range(CT):
                        col = (tt % 2) * C + ct * P
                        last = nc.tensor.transpose(ps[:, 4 + (tt // 2 + 2) % 4, col:col + P],
                                                   res[:, ct, tt * P:(tt + 1) * P], ident())
                    if tt % 2:
                        last.then_inc(t_full, 1)

            tokens(0, 0)
            with pe.Fori(0, B) as b:
                def layer_norm(i):
                    if i == 1:
                        tokens(b, 1)
                        conv_q(b + 1)
                        conv_vk(0)
                    pe.wait_ge(n_act, b * 4 + 2 * i + 2)
                    pe.wait_ge(n_dve, b * 4 + 2 * i + 2)
                    for k in range(4):
                        if i and k == 1:
                            pe.wait_ge(q_ready, b + 2)
                        if i and k == 2:
                            pe.wait_ge(vk_ready, b * NH + NH + 1)
                        if i == 0 and k == 2:
                            pe.wait_ge(f_out, b * NH * CT + CT)
                        for q in range(4):
                            tt = 4 * (k // 2) + q
                            last = nc.tensor.transpose(ps[:, back_bank(i, k), q * P:(q + 1) * P],
                                                       xt[:, tt, (k % 2) * P:(k % 2 + 1) * P], ident())
                        last.then_inc(back_full, 1)

                layer_norm(0)
                def ring_step(item):
                    n = RING_AT[item]
                    if n >= 2:
                        pe.wait_ge(ring_free, b * len(RING) + n - 1)
                    slot = wide(n % 2)
                    if item[0] == "proj":
                        g, t = divmod(item[1], 4)
                        for half in range(NH):
                            if item[1] == 0:
                                pe.wait_ge(back_lo, b * 8 + 2 * half + 2)
                            last = split_mm(slot[:, half, :], W_QK + t * CT * C + g * P, (C, P),
                                            slice(half * HALF, (half + 1) * HALF))
                    elif item[0] == "score":
                        _, u, q = item
                        s = u % NST
                        if q == 0:
                            pe.wait_ge(stack_in[s], (b * SLOT_USES[s] + u // NST + 1) * STACK_DMAS * 16)
                        for half in range(NH):
                            last = mm(slot[:, half, :], stack[0:AUX, s, 0, q * P:(q + 1) * P],
                                      stack[0:AUX, s, 1, half * HALF:(half + 1) * HALF], start=True, stop=True)
                    else:
                        u = item[1]
                        pe.wait_ge(ring_free, b * len(RING) + RING_AT["score", u, NT - 1] + 1)
                        last = nc.tensor.transpose(slot[0:NT, 0, 0:P], nm[:, u % 2, :], ident())
                    last.then_inc(ring_full, 1)

                def weighted(u, kt):
                    h, k, bank = u // 2, u * NT + kt, 6 + u % 2
                    pe.wait_ge(p_ready, b * 2 * UNITS * NT + 2 * k + 2)
                    if kt == 0 and u >= 2:
                        pe.wait_ge(o_free, b * UNITS + u - 1)
                    for c in range(4):
                        last = mm(ps[HD * c:HD * c + HD, bank, 0:CQ], vt[:, kt, HD * h:HD * h + HD],
                                  probs[:, k % NP, c * CQ:(c + 1) * CQ], start=(kt == 0),
                                  stop=(kt == NT - 1), skip_group_check=True)
                    last.then_inc(pv_done, 1)

                def ones_mm(u, tile, last):
                    for c in range(4):
                        ins = mm(ps[HD * c:HD * c + HD, 6 + u % 2, CQ:2 * CQ], ones[:, :],
                                 tile[:, c * CQ:(c + 1) * CQ], start=False, stop=last, skip_group_check=True)
                    return ins

                def add_up(n):
                    made = b * ADDS + adds(min(QUAD * n + QUAD, ADDED) - 1)
                    pe.wait_ge(sum_pool, made)
                    pe.wait_ge(sum_dve, made)
                    u, quad = divmod(n, QUADS)
                    ins = ones_mm(u, psums[:, n % NS, :], quad == QUADS - 1 and u < UNITS - 1)
                    if n < UNITS * QUADS - 1:
                        ins.then_inc(ones_done, 1)

                def values(tt):
                    n = 0
                    for kt in range(CT):
                        for xx, wt in ((xh, wh), (xh, wl), (xl, wh)):
                            last = mm(ps[:, 4 + tt // 2, (tt % 2) * C:(tt % 2 + 1) * C], xx[:, kt, tt * P:(tt + 1) * P],
                                      wt[:, W_V + kt * C:W_V + (kt + 1) * C], start=(n == 0), stop=(n == 5))
                            n += 1
                    if tt % 2:
                        last.then_inc(v_full, 1)

                for item in BEFORE:
                    ring_step(item)
                    if item[0] == "score" and item[1] == 0:
                        values(item[2])
                pe.wait_ge(v_ready, b * 4 + 4)
                for u in range(UNITS):
                    s = u % NST
                    pe.wait_ge(aux_in[s], (b * SLOT_USES[s] + u // NST + 1) * AUX_DMAS * 16)
                    for kt in range(NT):
                        k = u * NT + kt
                        for half in range(NH):
                            if k >= 1:
                                pe.wait_ge(p_ready, b * 2 * UNITS * NT + 2 * k + half - 1)
                            mm(ps[:, 4 + half, :], stack[0:KS, s, 1, kt * P:(kt + 1) * P],
                               stack[0:KS, s, 0, half * HALF:(half + 1) * HALF], start=True,
                               stop=True).then_inc(st_full, 1)
                        for item in BESIDE[u, kt]:
                            ring_step(item)
                        if k >= 1:
                            weighted(*divmod(k - 1, NT))
                        if k >= ADD_AT and (k - ADD_AT) % QUAD == 0:
                            add_up((k - ADD_AT) // QUAD)
                weighted(UNITS - 1, NT - 1)
                add_up(UNITS * QUADS - 1)
                for k in range(ADDED, UNITS * NT):
                    last = ones_mm(UNITS - 1, probs[:, k % NP, :], k == UNITS * NT - 1)
                last.then_inc(ones_done, 1)

                pe.wait_ge(g_stat, b + 1)
                mm(ps[:, 0, 0:8], wf[:, F_BLK:F_BLK + P], small[:, 88:96], start=True, stop=True).then_inc(g_full, 1)
                for k in range(4):
                    half = k // 2
                    pe.wait_ge(on_lo, b * NH * CT + CT * half + CT)
                    split_mm(ps[:, k, :], W_O + (k % 2) * P, (C, P),
                             slice(half * HALF, (half + 1) * HALF)).then_inc(y1_full, 1)
                layer_norm(1)

                for half in range(NH):
                    pe.wait_ge(back_lo, b * 8 + 4 + 2 * half + 2)
                    last = split_mm(ps[:, half, :], W_R, (E, P), slice(half * HALF, (half + 1) * HALF))
                last.then_inc(r_full, 1)
                pe.wait_ge(r_rows, b + 1)
                nc.tensor.transpose(ps[:, 0, 0:P], lrow[:, 0:P], ident())
                for tt in range(1, NT):
                    last = nc.tensor.transpose(ps[:, 0, tt * E:(tt + 1) * E], lrow[0:E, tt * P:(tt + 1) * P],
                                               wf[0:E, F_ID:F_ID + E])
                last.then_inc(r_full, 1)

                def down(i):
                    half, e = divmod(i, NE)
                    pe.wait_ge(f_lo, b * NH * NE + i + 1)
                    if e == 0 and half:
                        pe.wait_ge(f_out, b * NH * CT + 2 * CT)
                    for t in range(CT):
                        col = W_DOWN + e * C + t * P
                        for n, (wt, hx) in enumerate(((wh, hh), (wl, hh), (wh, hl))):
                            last = mm(ps[:, t, :], wt[:, col:col + P], hx[:, i % 2, :],
                                      start=(e == 0 and n == 0), stop=(e == NE - 1 and n == 2))
                    last.then_inc(f_down, 1)

                for i in range(NH * NE):
                    half, e = divmod(i, NE)
                    cols = slice(half * HALF, (half + 1) * HALF)
                    if i == 2:
                        pe.wait_ge(vk_ready, b * NH + 2 * NH)
                    if i == NE + 1:
                        conv_scores(b + 1)
                    if i >= 2:
                        pe.wait_ge(f_hid, b * NH * NE + i - 1)
                    bank = 2 + 3 * (i % 2)
                    for part in range(2):
                        last = split_mm(ps[:, bank + part, :], W_GU + (2 * e + part) * CT * HID, (HID, HID), cols)
                    if i == 1:
                        pe.wait_ge(r_comb, b + 1)
                        for tt in range(NT):
                            last = nc.tensor.transpose(ps[0:E, tt // 4, (tt % 4) * P:(tt % 4 + 1) * P],
                                                       route[:, 5, tt * E:(tt + 1) * E], ident())
                        last.then_inc(cb_full, 1)
                        conv_vk(1)
                        pe.wait_ge(cb_lo, b + 1)
                    if i == NE + 2:
                        pe.wait_ge(a2_ready, b + 2)
                    if e:
                        last = mm(ps[:, bank + 2, :], wh[:, W_SEL + e - 1:W_SEL + e].broadcast_to([P, P]), comb_t[:, cols],
                                  start=True, stop=True)
                    last.then_inc(f_full, 1)
                    if i == NE + 1:
                        conv_wo(b + 1)
                    if i >= 2:
                        down(i - 2)
                pe.wait_ge(f_hid, b * NH * NE + NH * NE - 1)
                for k in range(3):
                    conv_last(k)
                pe.wait_ge(f_hid, b * NH * NE + NH * NE)
                conv_last(3)
                tokens(b + 1, 0)
                down(NH * NE - 2)
                pe.wait_ge(t_var, b * 2 + 3)
                down(NH * NE - 1)


def kernel(**inputs):
    import concourse.bacc as bacc
    from concourse.bass_utils import run_bass_kernel_spmd

    a = {k: np.asarray(v) for k, v in inputs.items()}

    def by_rows(w):
        return w.reshape(CT, P, -1).transpose(1, 0, 2).reshape(P, -1)

    def spread(vec):
        return np.broadcast_to(vec.reshape(1, -1), (P, vec.size))

    def column(vec):
        return vec.reshape(-1, P).T

    def pad(w):
        return np.concatenate([w, np.zeros((P - w.shape[0], w.shape[1]), np.float32)])

    L0, L1, L2 = "L0_conv_", "L1_attn_", "L1_ffn_"
    parts = [by_rows(a[L1 + n].T) for n in ("Q1_w", "K1_w", "Q2_w", "K2_w", "V_w", "out_w")]
    parts.append(by_rows(a[L2 + "router"]))
    parts += [by_rows(a[L2 + "shared_gate"]), by_rows(a[L2 + "shared_up"])]
    for e in range(E):
        parts += [by_rows(a[L2 + "W_gate"][e]), by_rows(a[L2 + "W_up"][e])]
    parts += [a[L2 + "shared_down"]] + [a[L2 + "W_down"][e] for e in range(E)]
    sel = np.zeros((P, E), np.float32)
    for e in range(E):
        sel[e, e] = sel[32 + e, e] = 0.5
    parts.append(sel)
    w_split = np.ascontiguousarray(np.concatenate(parts, 1))

    qvk = np.concatenate([a[L0 + "Wq"].T, a[L0 + "Wv"].T, a[L0 + "Wk"].T], 1)
    blk = np.full((P, P), 1 / (4 * P), np.float32)
    idx = np.tile(E - np.arange(E, dtype=np.float32), (P, NT))
    full = [by_rows(qvk)]
    full += [pad(a[L0 + "Wo"].T), np.eye(P, dtype=np.float32), blk, idx]
    full += [pad(np.concatenate([a[L0 + "bv"], a[L0 + "bk"]])[:, None]), column(a[L0 + "bo"]),
             spread(a[L0 + "gamma"]), column(a[L1 + "K1_b"]), column(a[L1 + "K2_b"]), column(a[L1 + "gn_w"]),
             column(a[L1 + "gn_b"]), column(a[L1 + "out_b"])]
    full += [spread(a[L1 + "lambda_" + n]) for n in ("q1", "k1", "q2", "k2")] + [spread(a[L0 + "bq"])]
    w_full = np.ascontiguousarray(np.concatenate(full, 1))

    arrays = {"x_dram": np.ascontiguousarray(a["x"].reshape(B, C, N)), "w_split_dram": w_split,
              "w_full_dram": w_full}
    nc = bacc.Bacc("TRN2", target_bir_lowering=False, num_devices=1)
    args = [nc.dram_tensor(k, w.shape, mybir.dt.from_np(w.dtype), kind="ExternalInput").ap()
            for k, w in arrays.items()]
    out = nc.dram_tensor("y_dram", (B, C, N), F32, kind="ExternalOutput").ap()
    build(nc, *args, out)
    r = run_bass_kernel_spmd(nc, [arrays], core_ids=[0])
    return r.results[0]["y_dram"].reshape(B, C, 32, 32)
```
